# Optimizing a Trainium2 kernel written in Bass

```python
import numpy as np
import jax
import jax.numpy as jnp

def _softmax(x, axis=-1):
    return jax.nn.softmax(x, axis=axis)

def _gelu(x):
    return jax.nn.gelu(x, approximate=True)

def _silu(x):
    return jax.nn.silu(x)

def _sigmoid(x):
    return jax.nn.sigmoid(x)

def _layernorm(x, axis=-1, eps=1e-05):
    m = jnp.mean(x, axis=axis, keepdims=True)
    v = jnp.var(x, axis=axis, keepdims=True)
    return (x - m) / jnp.sqrt(v + eps)

def _scatter_add(tgt, idx, src, axis=0):
    return tgt.at[idx].add(src)

def _segment_sum(src, seg, n):
    return jax.ops.segment_sum(src, seg, n)
kernel_name = 'mk_flamingo_gated_d1_seqx_r8_214b67'

def setup_inputs(seed: int=0):
    np.random.seed(seed)
    _w = jnp.asarray

    def _rec_inputs():
        import jax
        import jax.numpy as jnp
        _rk = jax.random.key(seed)
        x = -0.0002928 + 1 * jax.random.normal(jax.random.fold_in(_rk, 1), (32, 64, 256), jnp.float32)
        _lenS = 64 - jax.random.randint(jax.random.fold_in(_rk, 7), (32,), 0, max(1, 64 // 4) + 1, jnp.int32)
        _lenS2 = 64 - jax.random.randint(jax.random.fold_in(_rk, 8), (32,), 0, max(1, 64 // 4) + 1, jnp.int32)
        _ctx_2048P = jax.random.normal(jax.random.fold_in(_rk, 11), (32, 16, 256), jnp.float32)
        _ctx_2048c = jax.random.dirichlet(jax.random.fold_in(_rk, 511), 0.3 * jnp.ones((16,), jnp.float32), (32, 64))
        _ctx_2048t = jnp.einsum('bsk,bkd->bsd', _ctx_2048c, _ctx_2048P)
        _ctx_2048t = _ctx_2048t * jax.lax.rsqrt(jnp.mean(jnp.square(_ctx_2048t)) + 1e-12) * 0.953939
        ctx_2048 = -1.39393e-06 + 0.999914 * (_ctx_2048t + 0.3 * jax.random.normal(jax.random.fold_in(_rk, 611), (32, 64, 256), jnp.float32))
        _g = jax.random.normal(jax.random.fold_in(_rk, 9001), (2, 1), jnp.float32)
        _g = jnp.sign(_g) * jnp.maximum(jnp.abs(_g), 1.0) + (_g == 0) * 1.0
        g_xattn = _g[0]
        g_ffn = _g[1]
        return (x, ctx_2048, g_xattn, g_ffn)
    x, ctx_2048, g_xattn, g_ffn = _rec_inputs()

    def _L0_xattn_setup():
        import jax, jax.numpy as jnp
        import numpy as np
        HEADS = 8
        DIM_HEAD = 64
        HIDDEN = HEADS * DIM_HEAD
        key = jax.random.key(seed)
        ks = jax.random.split(key, 5)
        b, dim, n = (4, 64, 256)
        ctx_dim, m = (64, 256)
        x = jax.random.normal(ks[0], (b, dim, n), dtype=jnp.float32)
        context = jax.random.normal(ks[1], (b, ctx_dim, m), dtype=jnp.float32)
        Wq = jax.random.normal(ks[2], (HIDDEN, dim), dtype=jnp.float32) / np.sqrt(dim).astype(np.float32)
        Wkv = jax.random.normal(ks[3], (2 * HIDDEN, ctx_dim), dtype=jnp.float32) / np.sqrt(ctx_dim).astype(np.float32)
        Wout = jax.random.normal(ks[4], (dim, HIDDEN), dtype=jnp.float32) / np.sqrt(HIDDEN).astype(np.float32)
        bout = jnp.zeros((dim,), dtype=jnp.float32)
        return {'x': x, 'context': context, 'Wq': Wq, 'Wkv': Wkv, 'Wout': Wout, 'bout': bout}
    _L0_xattn_all = _L0_xattn_setup()
    _L0_xattn_in = {k: v for k, v in _L0_xattn_all.items() if k in ('Wq', 'Wkv', 'Wout', 'bout')}
    del _L0_xattn_all

    def _L0_ffn_setup():
        import jax, jax.numpy as jnp
        import numpy as np
        B, S, DIM = (2, 256, 256)
        INTER = 128
        E = 8
        K = 2
        N_SHARED = 1
        ROUTE_SCALE = 1.0
        key = jax.random.key(seed)
        ks = jax.random.split(key, 8)
        s_in = 1.0 / np.sqrt(DIM)
        s_hid = 1.0 / np.sqrt(INTER)
        return {'x': jax.random.normal(ks[0], (B, S, DIM), dtype=jnp.float32), 'gate_w': jax.random.normal(ks[1], (E, DIM), dtype=jnp.float32) * s_in, 'w1': jax.random.normal(ks[2], (E, INTER, DIM), dtype=jnp.float32) * s_in, 'w2': jax.random.normal(ks[3], (E, DIM, INTER), dtype=jnp.float32) * s_hid, 'w3': jax.random.normal(ks[4], (E, INTER, DIM), dtype=jnp.float32) * s_in, 'ws1': jax.random.normal(ks[5], (N_SHARED * INTER, DIM), dtype=jnp.float32) * s_in, 'ws2': jax.random.normal(ks[6], (DIM, N_SHARED * INTER), dtype=jnp.float32) * s_hid, 'ws3': jax.random.normal(ks[7], (N_SHARED * INTER, DIM), dtype=jnp.float32) * s_in}
    _L0_ffn_all = _L0_ffn_setup()
    _L0_ffn_in = {k: v for k, v in _L0_ffn_all.items() if k in ('gate_w', 'w1', 'w2', 'w3', 'ws1', 'ws2', 'ws3')}
    del _L0_ffn_all
    return {'x': x, 'ctx_2048': ctx_2048, 'g_xattn': g_xattn, 'g_ffn': g_ffn, 'L0_xattn_Wq': _L0_xattn_in['Wq'], 'L0_xattn_Wkv': _L0_xattn_in['Wkv'], 'L0_xattn_Wout': _L0_xattn_in['Wout'], 'L0_xattn_bout': _L0_xattn_in['bout'], 'L0_ffn_gate_w': _L0_ffn_in['gate_w'], 'L0_ffn_w1': _L0_ffn_in['w1'], 'L0_ffn_w2': _L0_ffn_in['w2'], 'L0_ffn_w3': _L0_ffn_in['w3'], 'L0_ffn_ws1': _L0_ffn_in['ws1'], 'L0_ffn_ws2': _L0_ffn_in['ws2'], 'L0_ffn_ws3': _L0_ffn_in['ws3']}

def reference(x, ctx_2048, g_xattn, g_ffn, L0_xattn_Wq, L0_xattn_Wkv, L0_xattn_Wout, L0_xattn_bout, L0_ffn_gate_w, L0_ffn_w1, L0_ffn_w2, L0_ffn_w3, L0_ffn_ws1, L0_ffn_ws2, L0_ffn_ws3):
    import jax
    import jax.numpy as jnp

    def _L0_xattn_ref(x, context, Wq, Wkv, Wout, bout):
        import jax, jax.numpy as jnp
        import numpy as np
        HEADS = 8
        DIM_HEAD = 64
        HIDDEN = HEADS * DIM_HEAD
        b = x.shape[0]
        q = jnp.einsum('oc,bcn->bon', Wq, x)
        kv = jnp.einsum('oc,bcm->bom', Wkv, context)
        k, v = jnp.split(kv, 2, axis=1)
        split_heads = lambda t: t.reshape(b, HEADS, DIM_HEAD, t.shape[-1])
        q, k, v = (split_heads(q), split_heads(k), split_heads(v))
        sim = jnp.einsum('bhdi,bhdj->bhij', q, k)
        attn = jax.nn.softmax(sim, axis=-1)
        out = jnp.einsum('bhij,bhdj->bhid', attn, v)
        out = jnp.transpose(out, (0, 1, 3, 2)).reshape(b, HIDDEN, -1)
        return jnp.einsum('oc,bcn->bon', Wout, out) + bout[None, :, None]

    def _L0_ffn_ref(x, gate_w, w1, w2, w3, ws1, ws2, ws3):
        import jax, jax.numpy as jnp
        import numpy as np
        B, S, DIM = (2, 256, 256)
        INTER = 128
        E = 8
        K = 2
        N_SHARED = 1
        ROUTE_SCALE = 1.0
        shape = x.shape
        xf = x.reshape(-1, DIM)
        scores = jax.nn.softmax(xf @ gate_w.T, axis=-1)
        weights, idx = jax.lax.top_k(scores, K)
        weights = weights * ROUTE_SCALE
        h = jnp.einsum('td,eid->eti', xf, w1)
        g = jax.nn.silu(h) * jnp.einsum('td,eid->eti', xf, w3)
        eo = jnp.einsum('eti,edi->etd', g, w2)
        comb = jnp.einsum('tke,tk->te', jax.nn.one_hot(idx, E, dtype=xf.dtype), weights)
        y = jnp.einsum('etd,te->td', eo, comb)
        z = jax.nn.silu(xf @ ws1.T) * (xf @ ws3.T) @ ws2.T
        return (y + z).reshape(shape)
    x = x + jnp.tanh(g_xattn[0]) * _L0_xattn_ref(_layernorm(x, axis=-1), ctx_2048, L0_xattn_Wq, L0_xattn_Wkv, L0_xattn_Wout, L0_xattn_bout)
    x = x + jnp.tanh(g_ffn[0]) * _L0_ffn_ref(_layernorm(x, axis=-1), L0_ffn_gate_w, L0_ffn_w1, L0_ffn_w2, L0_ffn_w3, L0_ffn_ws1, L0_ffn_ws2, L0_ffn_ws3)
    return x

_drawn_inputs = setup_inputs


def setup_inputs(seed=0):
    import zlib

    import numpy as np

    out = dict(_drawn_inputs(seed))
    spreads = {'L0_xattn_bout': (0.0, 0.1)}
    factors = {}
    for name, (base, spread) in spreads.items():
        noise = np.random.default_rng([zlib.crc32(name.encode()), seed]).standard_normal(out[name].shape)
        drawn = base * np.exp(spread * noise) if base else spread * noise
        out[name] = jnp.asarray(drawn.astype(out[name].dtype))
    for name, factor in factors.items():
        out[name] = (out[name] * factor).astype(out[name].dtype)
    return out
```

```python
from contextlib import ExitStack

import numpy as np

import concourse.bass as bass
from concourse import mybir

F32 = mybir.dt.float32
F32R = mybir.dt.float32r
ALU = mybir.AluOpType
ACT = mybir.ActivationFunctionType
AX = mybir.AxisListType

P = 128
B, C, N = 32, 64, 256
HEADS, DH = 8, 64
E_ROUTED, INTER = 8, 128
EXPERTS = E_ROUTED + 1
D = N
PAIRS = B // 2
JB = N // P
DB = D // P
EPS = 1e-5
CHUNK = 512
TILES = CHUNK // P
CHUNKS = B * C // CHUNK
W_COLS = EXPERTS * (2 * DB * INTER + D)
W_STEP = W_COLS // B

RING = ["G0", "G1", "U0", "G2", "G3", "S0", "S1", "S2", "S3", "U1", "S4", "S5", "S6", "S7"]
RN = len(RING)

K_ID, K_HEAD, K_PAIR, K_FOLD, K_DEN, K_RANK = 0, 128, 136, 648, 712, 776
K_COLS = 784


def constants():
    k = np.zeros((P, K_COLS), np.float32)
    k[:, K_ID:K_ID + P] = np.eye(P)
    for h in range(HEADS):
        k[C + h, K_HEAD + h] = 1
        row = 32 * (h % 4) + h // 4
        at = K_PAIR + P * (h // 2) + C * (h % 2)
        k[row, at:at + C] = 1
    k[:, K_FOLD:K_FOLD + C] = np.vstack([np.eye(C), np.eye(C)])
    k[:, K_DEN:K_DEN + 32] = 1
    k[:, K_DEN + 1] = 0
    k[:, K_DEN + 32 + 1] = 1
    k[:, K_RANK:K_RANK + E_ROUTED] = E_ROUTED - np.arange(E_ROUTED)
    return k


def need(eng, sem, value):
    if not isinstance(value, int) or value > 0:
        eng.wait_ge(sem, value)


def build(nc, x, ctx_in, g_xattn, g_ffn, wq, wk, wv, woT, bout, gateT, w_all, consts, out):
    with ExitStack() as stack:
        def sb(name, shape, dt=F32):
            return stack.enter_context(nc.sbuf_tensor(name, shape, dt))

        def bank(name):
            return stack.enter_context(nc.psum_tensor(name, [P, 512], F32))

        def sem(name):
            return stack.enter_context(nc.semaphore(name))

        kst = sb("kst", [P, K_COLS])
        ident_r = sb("ident_r", [P, P], F32R)
        pair_r = sb("pair_r", [P, HEADS // 2, P], F32R)
        mhl = sb("mhl", [P, HEADS, P], F32R)
        nhl = sb("nhl", [P, HEADS, C], F32R)
        gates = sb("gates", [P, 2])
        tg = sb("tg", [P, 2])
        bo = sb("bo", [P, 1])
        tgb = sb("tgb", [P, 1])
        hgf = sb("hgf", [P, 1])
        minus_half = sb("minus_half", [P, 1])
        eps = sb("eps", [P, 1])
        zero = sb("zero", [P, 1])
        gate_t = sb("gate_t", [P, DB, E_ROUTED])
        w_raw = [sb(f"w_raw{q}", [P, W_STEP]) for q in range(2)]
        w_hi = sb("w_hi", [P, W_COLS], F32R)
        w_lo = sb("w_lo", [P, W_COLS], F32R)
        x1 = sb("x1", [P, PAIRS, D])
        bn6t = sb("bn6t", [P, 6])
        mvt = sb("mvt", [P, 2])
        vet = sb("vet", [P, 1])
        rstdt = sb("rstdt", [P, 1])
        xn2 = sb("xn2", [P, D])
        xt = sb("xt", [P, DB, P])
        xth = sb("xth", [P, DB, B * C], F32R)
        xtl = sb("xtl", [P, DB, B * C], F32R)
        logit = sb("logit", [P, PAIRS, E_ROUTED])
        comb = sb("comb", [P, PAIRS, EXPERTS])

        attention = stack.enter_context(ExitStack())

        def attn_sb(name, shape, dt=F32):
            return attention.enter_context(nc.sbuf_tensor(name, shape, dt))

        raw_x = [attn_sb(f"raw_x{q}", [P, N]) for q in range(2)]
        raw_c = [attn_sb(f"raw_c{q}", [P, N]) for q in range(2)]
        bn6 = [attn_sb(f"bn6_{q}", [P, 6]) for q in range(2)]
        mv = [attn_sb(f"mv{q}", [P, 2]) for q in range(2)]
        ve = [attn_sb(f"ve{q}", [P, 1]) for q in range(2)]
        rstd = [attn_sb(f"rstd{q}", [P, 1]) for q in range(2)]
        xn = attn_sb("xn", [C, N])
        xh = [attn_sb(f"xh{q}", [P, N], F32R) for q in range(2)]
        xlm = [attn_sb(f"xlm{q}", [P, N], F32R) for q in range(2)]
        ch = [attn_sb(f"ch{q}", [P, N], F32R) for q in range(2)]
        cl = [attn_sb(f"cl{q}", [P, N], F32R) for q in range(2)]
        ghl = [attn_sb(f"ghl{q}", [P, HEADS, N], F32R) for q in range(2)]
        ghs = [attn_sb(f"ghs{q}", [P, HEADS, N], F32R) for q in range(2)]
        u = [attn_sb(f"u{q}", [P, JB, HEADS, C]) for q in range(2)]
        nmax = attn_sb("nmax", [P, JB, P], F32R)
        ex = [attn_sb(f"ex{h}", [P, JB, N]) for h in range(HEADS)]
        wq2, wk2, wv2 = (ex[h].rearrange("p b (k c) -> p (b k) c", c=2 * C).rearrange("p k (r c) -> p k r c", r=2) for h in range(3))
        wo = ex[3][:, 0, :].rearrange("p (k c) -> p k c", c=C)
        os_ = [attn_sb(f"os{q}", [P, HEADS // 2, N]) for q in range(2)]
        rz = attn_sb("rz", [P, N])
        rzh = attn_sb("rzh", [P, N], F32R)
        rzl = attn_sb("rzl", [P, N], F32R)
        acc = attn_sb("acc", [P, N])
        xr = attn_sb("xr", [P, N])
        ps = [bank("ps0"), bank("ps1")]
        pt = [bank("pt0"), bank("pt1")]
        po = [bank("po0"), bank("po1")]
        pz, pm = bank("pz"), bank("pm")

        setup_in = sem("setup_in")
        small_in = sem("small_in")
        w_in = [sem(f"w_in{q}") for q in range(2)]
        consts_done = sem("consts_done")
        zero_done = sem("zero_done")
        tanh_done = sem("tanh_done")
        tg_done = sem("tg_done")
        mprod_done = sem("mprod_done")
        mhi_done = sem("mhi_done")
        mhl_done = sem("mhl_done")
        x_in = [sem(f"x_in{q}") for q in range(2)]
        c_in = [sem(f"c_in{q}") for q in range(2)]
        xr_in = sem("xr_in")
        bn_done = sem("bn_done")
        stats_done = sem("stats_done")
        ve_done = sem("ve_done")
        rstd_done = sem("rstd_done")
        xh_done = sem("xh_done")
        xn_done = sem("xn_done")
        xl_done = sem("xl_done")
        ch_done = sem("ch_done")
        cl_done = sem("cl_done")
        ring_filled = sem("ring_filled")
        gh_done = sem("gh_done")
        gs_done = sem("gs_done")
        gl_done = sem("gl_done")
        u_done = sem("u_done")
        max_done = sem("max_done")
        mt_filled = sem("mt_filled")
        mt_done = sem("mt_done")
        st_done = sem("st_done")
        exp_done = sem("exp_done")
        av_done = sem("av_done")
        z_done = sem("z_done")
        os_done = sem("os_done")
        recip_done = sem("recip_done")
        rzh_done = sem("rzh_done")
        rzl_done = sem("rzl_done")
        rb_done = sem("rb_done")
        mul_done = sem("mul_done")
        add_done = sem("add_done")
        sum_done = sem("sum_done")
        y_done = sem("y_done")
        xr_done = sem("xr_done")
        res_done = sem("res_done")
        bnt_done = sem("bnt_done")
        statt_done = sem("statt_done")
        vet_done = sem("vet_done")
        rstdt_done = sem("rstdt_done")
        xn2_done = sem("xn2_done")
        tr_done = sem("tr_done")
        xt_done = sem("xt_done")
        xth_done = sem("xth_done")
        xtl_done = sem("xtl_done")
        lg_filled = sem("lg_filled")
        lg_done = sem("lg_done")
        wh_done = sem("wh_done")
        wl_done = sem("wl_done")
        rt_done = sem("rt_done")
        rexp_done = sem("rexp_done")
        comb_done = sem("comb_done")
        hu_filled = sem("hu_filled")
        th_done = sem("th_done")
        hs_done = sem("hs_done")
        g_done = sem("g_done")
        ghi_done = sem("ghi_done")
        glo_done = sem("glo_done")
        y2_filled = sem("y2_filled")
        y2_done = sem("y2_done")
        out_done = sem("out_done")

        def body_loop(eng, step, finish):
            step(0, 0)
            step(0, 1)
            with eng.Fori(1, PAIRS - 1) as it:
                step(it, 0)
                step(it, 1)
            step(PAIRS - 1, 0)
            step(PAIRS - 1, 1)
            finish()

        def known(v, limit):
            return not isinstance(v, int) or v < limit

        block = attention.enter_context(nc.Block())

        @block.sync
        def _(sp):
            def load(b, q, b_after):
                need(sp, xn_done, b_after)
                for r in (0, C):
                    sp.dma_start(raw_x[q][r:r + C, :], x[bass.ds(b, 1), :, :].rearrange("o c n -> (o c) n")).then_inc(x_in[q], 16)
                need(sp, cl_done, b_after)
                for r in (0, C):
                    sp.dma_start(raw_c[q][r:r + C, :], ctx_in[bass.ds(b, 1), :, :].rearrange("o c n -> (o c) n")).then_inc(c_in[q], 16)

            for t, w in ((wq2, wq), (wk2, wk), (wv2, wv)):
                for r in range(2):
                    sp.dma_start(t[:, :, r, :], w.rearrange("(k p) c -> p k c", p=P)).then_inc(setup_in, 16)
            sp.dma_start(wo[:, :, :], woT.rearrange("(k p) c -> p k c", p=P)).then_inc(setup_in, 16)
            sp.dma_start(kst[:, :], consts).then_inc(setup_in, 16)
            load(0, 0, 0)
            load(1, 1, 0)
            for t, g in enumerate((g_xattn, g_ffn)):
                sp.dma_start(gates[:, t:t + 1], g.rearrange("(a o) -> a o", a=1).broadcast_to([P, 1])).then_inc(small_in, 16)
            for r in (0, C):
                sp.dma_start(bo[r:r + C, :], bout.rearrange("(c o) -> c o", o=1)).then_inc(small_in, 16)
            sp.dma_start(gate_t[:, :, :], gateT.rearrange("(k p) e -> p k e", p=P)).then_inc(small_in, 16)

            def step(it, p):
                s = 2 * it + p
                need(sp, wl_done, s - 1)
                sp.dma_start(w_raw[p][:, :], w_all[:, bass.ds(s * W_STEP, W_STEP)]).then_inc(w_in[p], 16)
                if known(s + 2, B):
                    load(s + 2, p, s + 1)
                if p == 0:
                    need(sp, res_done, 2 * it)
                    sp.dma_start(xr[:, :], x[bass.ds(2 * it, 2), :, :].rearrange("b c n -> (b c) n")).then_inc(xr_in, 16)

            body_loop(sp, step, lambda: None)

        @block.tensor
        def _(pe):
            pe.wait_ge(setup_in, 16 * 8)
            for h in range(HEADS):
                r, k = DH * (h % 2), h // 2
                pe.matmul(ps[h % 2][:, P * k:P * k + P], wk2[r:r + DH, k, :, :].rearrange("d r c -> d (r c)"),
                          wq2[r:r + DH, k, :, :].rearrange("d r c -> d (r c)"), start=True, stop=True)
            for h in range(HEADS):
                r, k = DH * (h % 2), h // 2
                mm = pe.matmul(pt[h % 2][:, C * k:C * k + C], wv2[r:r + DH, k, :, :].rearrange("d r c -> d (r c)"),
                               wo[r:r + DH, k, :], start=True, stop=True)
            mm.then_inc(mprod_done, 1)
            pe.wait_ge(mhl_done, 4)
            pe.wait_ge(consts_done, 3)
            pe.wait_ge(zero_done, 6)

            def ring(use, b, q):
                k = RING.index(use)
                bank_ = ps[k % 2]
                before, back = RING[(k - 2) % RN], b if k >= 2 else b - 1
                i = int(before[1])
                if before[0] == "G":
                    need(pe, gl_done, 4 * back + i + 1)
                    need(pe, gs_done, 4 * back + i + 1)
                elif before[0] == "U":
                    need(pe, u_done, 2 * back + i + 1)
                else:
                    need(pe, max_done, 8 * back + i + 1)
                i = int(use[1])
                if use[0] == "G":
                    need(pe, cl_done, b + 1)
                    for h in range(2):
                        pe.matmul(bank_[:, N * h:N * h + N], mhl[:, 2 * i + h, :], ch[q][:, :], start=True, stop=False)
                        mm = pe.matmul(bank_[:, N * h:N * h + N], mhl[:, 2 * i + h, :], cl[q][:, :], start=False, stop=True)
                elif use[0] == "U":
                    js = slice(P * i, P * i + P)
                    pe.matmul(bank_[:, :], ch[q][:, js], nhl[:, :, :].rearrange("p h c -> p (h c)"), start=True, stop=False)
                    mm = pe.matmul(bank_[:, :], cl[q][:, js], nhl[:, :, :].rearrange("p h c -> p (h c)"), start=False, stop=True)
                else:
                    need(pe, gl_done, 4 * b + i // 2 + 1)
                    need(pe, xh_done, b + 1)
                    for ib in range(JB):
                        mm = pe.matmul(bank_[:, N * ib:N * ib + N], xh[q][:, P * ib:P * ib + P], ghl[q][:, i, :], start=True, stop=True)
                mm.then_inc(ring_filled, 1)

            def max_rows(b, free_sem, free_at):
                need(pe, max_done, 8 * b + 8)
                need(pe, free_sem, free_at)
                for ib in range(JB):
                    mm = pe.matmul(pm[:, P * ib:P * ib + P], nmax[:, ib, :], ident_r[:, :], start=True, stop=True)
                mm.then_inc(mt_filled, 1)

            def scores(s, p, h):
                if h == 0:
                    need(pe, xl_done, s + 1)
                    need(pe, mt_done, s + 1)
                    need(pe, gs_done, 4 * s + 4)
                need(pe, exp_done, 8 * s + h - 1)
                for jb in range(JB):
                    js = slice(P * jb, P * jb + P)
                    pe.matmul(pt[h % 2][:, N * jb:N * jb + N], ghl[p][:, h, js], xh[p][:, :], start=True, stop=False)
                    mm = pe.matmul(pt[h % 2][:, N * jb:N * jb + N], ghs[p][:, h, js], xlm[p][:, :], start=False, stop=True)
                mm.then_inc(st_done, 1)

            def weighted(s, p, k):
                need(pe, exp_done, 8 * s + 2 * k + 2)
                need(pe, u_done, 2 * s + 2)
                need(pe, os_done, 4 * s + k - 1)
                for jb in range(JB):
                    for r in range(2):
                        h = 2 * k + r
                        mm = pe.matmul(po[k % 2][C * r:C * r + C, 0:N], u[p][:, jb, h, :], ex[h][:, jb, :],
                                       start=(jb == 0), stop=(jb == JB - 1))
                mm.then_inc(av_done, 1)

            def denominators(s, k):
                if k == 0:
                    need(pe, recip_done, s)
                for jb in range(JB):
                    for t in range(4):
                        mm = pe.matmul(pz[32 * t:32 * t + 32, 0:N], kst[:, K_DEN + 32 * k:K_DEN + 32 * k + 32],
                                       ex[4 * k + t][:, jb, :], start=(k == 0 and jb == 0), stop=(k == 1 and jb == JB - 1))
                mm.then_inc(z_done, 1)

            def spread(f, k):
                if k == 0:
                    need(pe, rzl_done, f + 1)
                    need(pe, mt_done, f + 2 if known(f + 1, B) else B)
                else:
                    need(pe, mul_done, 2 * f + 1)
                for r in range(2):
                    o = pm[:, N * r:N * r + N]
                    pe.matmul(o, pair_r[:, 2 * k + r, :], rzh[:, :], start=True, stop=False)
                    mm = pe.matmul(o, pair_r[:, 2 * k + r, :], rzl[:, :], start=False, stop=True)
                mm.then_inc(rb_done, 1)

            def fold(f, fp):
                need(pe, sum_done, f + 1)
                need(pe, mul_done, 2 * f + 2)
                pe.matmul(pm[C * fp:C * fp + C, 0:N], kst[:, K_FOLD:K_FOLD + C], acc[:, :], start=True, stop=True).then_inc(y_done, 1)

            def turn(pair, f):
                need(pe, xn2_done, pair + 1)
                need(pe, res_done, f + 1)
                for db in range(DB):
                    mm = pe.transpose(pm[:, P * db:P * db + P], xn2[:, P * db:P * db + P], kst[:, K_ID:K_ID + P])
                mm.then_inc(tr_done, 1)

            def route(pair):
                need(pe, xt_done, pair + 1)
                for db in range(DB):
                    mm = pe.matmul(pm[:, 0:E_ROUTED], xt[:, db, :], gate_t[:, db, :], start=(db == 0), stop=(db == DB - 1))
                mm.then_inc(lg_filled, 1)

            for use in RING:
                ring(use, 0, 0)
            max_rows(0, mhl_done, 0)

            def step(it, p):
                s, q = 2 * it + p, 1 - p
                n, f = s + 1, s - 1
                nxt = known(n, B)
                fin = not isinstance(s, int) or s > 0
                tok = p == 1 and (not isinstance(it, int) or it > 0)

                def r(*uses):
                    if nxt:
                        for use in uses:
                            ring(use, n, q)

                scores(s, p, 0)
                r("G0")
                scores(s, p, 1)
                r("G1", "U0")
                scores(s, p, 2)
                r("G2")
                if fin:
                    spread(f, 0)
                scores(s, p, 3)
                r("G3")
                weighted(s, p, 0)
                if fin:
                    spread(f, 1)
                r("S0")
                scores(s, p, 4)
                r("S1")
                scores(s, p, 5)
                r("S2")
                weighted(s, p, 1)
                denominators(s, 0)
                r("S3", "U1")
                scores(s, p, 6)
                if fin:
                    fold(f, q)
                r("S4")
                scores(s, p, 7)
                r("S5")
                if tok:
                    turn(it - 1, f)
                weighted(s, p, 2)
                r("S6", "S7")
                if tok:
                    route(it - 1)
                weighted(s, p, 3)
                if nxt:
                    if tok:
                        max_rows(n, lg_done, it)
                    else:
                        max_rows(n, res_done, s)
                denominators(s, 1)

            def finish():
                spread(B - 1, 0)
                spread(B - 1, 1)
                fold(B - 1, 1)
                turn(PAIRS - 1, B - 1)
                route(PAIRS - 1)

            body_loop(pe, step, finish)

        @block.scalar
        def _(act):
            act.wait_ge(mprod_done, 1)
            for r in range(2):
                act.activation(mhl[:, r:HEADS:2, :], ps[r][:, :].rearrange("p (k c) -> p k c", c=P), ACT.Copy).then_inc(mhi_done, 1)
            for r in range(2):
                act.activation(nhl[:, r:HEADS:2, :], pt[r][:, 0:4 * C].rearrange("p (k c) -> p k c", c=C), ACT.Copy).then_inc(mhi_done, 1)
            act.wait_ge(small_in, 16 * 5)
            act.activation(tg[:, :], gates[:, :], ACT.Tanh).then_inc(tanh_done, 1)

            def g_high(b, q, i):
                need(act, ring_filled, RN * b + RING.index(f"G{i}") + 1)
                src = ps[RING.index(f"G{i}") % 2]
                act.activation(ghl[q][:, 2 * i:2 * i + 2, :].rearrange("p h j -> p (h j)"), src[:, :], ACT.Copy).then_inc(gh_done, 1)
                act.activation(ghs[q][0:C, 2 * i:2 * i + 2, :].rearrange("p h j -> p (h j)"), src[0:C, :], ACT.Copy).then_inc(gs_done, 1)

            def u_out(b, q, i):
                need(act, ring_filled, RN * b + RING.index(f"U{i}") + 1)
                act.activation(u[q][:, i, :, :].rearrange("p h c -> p (h c)"), ps[RING.index(f"U{i}") % 2][:, :], ACT.Copy).then_inc(u_done, 1)

            def expo(s, h):
                need(act, st_done, 8 * s + h + 1)
                need(act, z_done, 2 * s - 1 + h // 4)
                act.activation(ex[h][:, :, :].rearrange("p b i -> p (b i)"), pt[h % 2][:, :], ACT.Exp).then_inc(exp_done, 1)

            def sums_out(s, p, k):
                need(act, av_done, 4 * s + k + 1)
                if k == 0:
                    need(act, sum_done, s - 1)
                act.activation(os_[p][:, k, :], po[k % 2][:, 0:N], ACT.Copy).then_inc(os_done, 1)

            def rz_high(f):
                need(act, recip_done, f + 1)
                need(act, rb_done, 2 * f)
                act.activation(rzh[:, :], rz[:, :], ACT.Copy).then_inc(rzh_done, 1)

            def turned(pair):
                need(act, tr_done, pair + 1)
                need(act, lg_filled, pair)
                need(act, xtl_done, pair)
                act.activation(xt[:, :, :].rearrange("p b t -> p (b t)"), pm[:, 0:D], ACT.Copy).then_inc(xt_done, 1)
                need(act, xt_done, pair + 1)
                act.activation(xth[:, :, bass.ds(P * pair, P)], xt[:, :, :], ACT.Copy).then_inc(xth_done, 1)

            for i, use in enumerate(RING):
                if use[0] == "G":
                    g_high(0, 0, int(use[1]))
                if use[0] == "U":
                    u_out(0, 0, int(use[1]))

            def step(it, p):
                s, q = 2 * it + p, 1 - p
                n, f = s + 1, s - 1
                nxt = known(n, B)
                fin = not isinstance(s, int) or s > 0
                tok = p == 1 and (not isinstance(it, int) or it > 0)
                expo(s, 0)
                if nxt:
                    g_high(n, q, 0)
                expo(s, 1)
                if nxt:
                    g_high(n, q, 1)
                if fin:
                    rz_high(f)
                if nxt:
                    u_out(n, q, 0)
                expo(s, 2)
                if nxt:
                    g_high(n, q, 2)
                expo(s, 3)
                if nxt:
                    g_high(n, q, 3)
                sums_out(s, p, 0)
                expo(s, 4)
                expo(s, 5)
                sums_out(s, p, 1)
                if nxt:
                    u_out(n, q, 1)
                expo(s, 6)
                expo(s, 7)
                if tok:
                    turned(it - 1)
                sums_out(s, p, 2)
                sums_out(s, p, 3)

            def finish():
                rz_high(B - 1)
                turned(PAIRS - 1)

            body_loop(act, step, finish)

        @block.vector
        def _(dve):
            dve.memset(nmax[:, :, :].bitcast(F32), 0.0).then_inc(zero_done, 1)
            for q in range(2):
                dve.memset(xlm[q][C:P, :].bitcast(F32), 0.0).then_inc(zero_done, 1)
            dve.wait_ge(setup_in, 16 * 8)
            dve.tensor_scalar(ident_r[:, :], kst[:, K_ID:K_ID + P], 1.0, None, ALU.mult).then_inc(consts_done, 1)
            dve.tensor_scalar(pair_r[:, :, :].rearrange("p k m -> p (k m)"), kst[:, K_PAIR:K_PAIR + 4 * P], 1.0, None, ALU.mult).then_inc(consts_done, 1)

            def stats(b, q, i):
                need(dve, x_in[q], 32 * i)
                dve.bn_stats(bn6[q][:, :], raw_x[q][:, :]).then_inc(bn_done, 1)

            def aggregate(b, q):
                dve.bn_aggr(mv[q][:, :], bn6[q][:, :]).then_inc(stats_done, 1)

            def norm(b, q):
                need(dve, rstd_done, b + 1)
                need(dve, st_done, 8 * (b - 1))
                dve.tensor_scalar(xh[q][:, :], raw_x[q][:, :], mv[q][:, 0:1], rstd[q][:, 0:1], ALU.subtract, ALU.mult).then_inc(xh_done, 1)
                need(dve, xl_done, b)
                dve.tensor_scalar(xn[:, :], raw_x[q][0:C, :], mv[q][0:C, 0:1], rstd[q][0:C, 0:1], ALU.subtract, ALU.mult).then_inc(xn_done, 1)

            for q in range(2):
                stats(q, q, 1)
                dve.wait_ge(bn_done, q + 1)
                aggregate(q, q)
            for q in range(2):
                sel = dve.tensor_copy(ghs[q][C:P, :, :], kst[C:P, K_HEAD:K_HEAD + HEADS].unsqueeze(2).broadcast_to([C, HEADS, N]))
            sel.then_inc(consts_done, 1)
            for t, (dst, src, w) in enumerate(((mhl, ps, P), (mhl, ps, P), (nhl, pt, C), (nhl, pt, C))):
                r = t % 2
                dve.wait_ge(mhi_done, t + 1)
                lo = dst[C:P, r:HEADS:2, :]
                dve.tensor_tensor(lo, src[r][C:P, 0:4 * w].rearrange("p (k c) -> p k c", c=w), lo.bitcast(F32), ALU.subtract).then_inc(mhl_done, 1)
            norm(0, 0)
            dve.wait_ge(tanh_done, 1)
            dve.tensor_tensor(tgb[:, :], tg[:, 0:1], bo[:, :], ALU.mult).then_inc(tg_done, 1)
            dve.tensor_scalar(hgf[:, :], tg[:, 1:2], 0.5, None, ALU.mult).then_inc(tg_done, 1)

            def g_low(b, q, i):
                need(dve, gh_done, 4 * b + i + 1)
                lo = ghl[q][C:P, 2 * i:2 * i + 2, :].rearrange("p h j -> p (h j)")
                dve.tensor_tensor(lo, ps[RING.index(f"G{i}") % 2][C:P, :], lo.bitcast(F32), ALU.subtract).then_inc(gl_done, 1)

            def maxima(b, h):
                k = RING.index(f"S{h}")
                need(dve, ring_filled, RN * b + k + 1)
                dve.tensor_reduce(nmax[:, :, C + h], ps[k % 2][:, :].rearrange("p (b j) -> p b j", j=N), AX.X, ALU.max, negate=True).then_inc(max_done, 1)

            def max_in(b, q):
                need(dve, mt_filled, b + 1)
                dve.tensor_copy(xlm[q][C:C + HEADS, :], pm[C:C + HEADS, 0:N]).then_inc(mt_done, 1)

            def recip(f):
                need(dve, z_done, 2 * f + 2)
                need(dve, rzl_done, f)
                dve.reciprocal(rz[:, :], pz[:, 0:N]).then_inc(recip_done, 1)

            def divide(f, fp, k):
                need(dve, rb_done, 2 * f + k + 1)
                need(dve, os_done, 4 * f + 2 * k + 2)
                o = os_[fp][:, 2 * k:2 * k + 2, :].rearrange("p k i -> p (k i)")
                dve.tensor_tensor(o, o, pm[:, :], ALU.mult).then_inc(mul_done, 1)

            def residual(f, fp, pair):
                need(dve, y_done, f + 1)
                need(dve, xr_done, pair + 1)
                rows = slice(C * fp, C * fp + C)
                dve.scalar_tensor_tensor(out=x1[rows, pair, :] if isinstance(pair, int) else x1[rows, bass.ds(pair, 1), :].rearrange("p o d -> p (o d)"),
                                         in0=pm[rows, 0:N], scalar=tg[rows, 0:1], in1=xr[rows, :], op0=ALU.mult, op1=ALU.add).then_inc(res_done, 1)

            def x1_of(pair):
                return x1[:, bass.ds(pair, 1), :].rearrange("p o d -> p (o d)")

            def token_stats(pair):
                need(dve, res_done, 2 * pair + 2)
                dve.bn_stats(bn6t[:, :], x1_of(pair)).then_inc(bnt_done, 1)

            def token_aggregate():
                dve.bn_aggr(mvt[:, :], bn6t[:, :]).then_inc(statt_done, 1)

            def token_norm(pair):
                need(dve, rstdt_done, pair + 1)
                need(dve, tr_done, pair)
                dve.tensor_scalar(xn2[:, :], x1_of(pair), mvt[:, 0:1], rstdt[:, 0:1], ALU.subtract, ALU.mult).then_inc(xn2_done, 1)

            def logits_out(pair):
                need(dve, lg_filled, pair + 1)
                dve.tensor_copy(logit[:, bass.ds(pair, 1), :].rearrange("p o e -> p (o e)"), pm[:, 0:E_ROUTED]).then_inc(lg_done, 1)

            def weights_high(s, it, p):
                cols = bass.ds(s * W_STEP, W_STEP)
                need(dve, w_in[p], 16 * (it + 1))
                dve.tensor_scalar(w_hi[:, cols], w_raw[p][:, :], 1.0, None, ALU.mult).then_inc(wh_done, 1)

            for use in RING:
                if use[0] == "G":
                    g_low(0, 0, int(use[1]))
                if use[0] == "S":
                    maxima(0, int(use[1]))
            max_in(0, 0)

            def step(it, p):
                s, q = 2 * it + p, 1 - p
                n, f = s + 1, s - 1
                nxt = known(n, B)
                fin = not isinstance(s, int) or s > 0
                late = not isinstance(it, int) or it > 0
                if nxt:
                    norm(n, q)
                if p == 1 and late:
                    token_norm(it - 1)
                if fin:
                    recip(f)
                if nxt:
                    for i in range(3):
                        g_low(n, q, i)
                if fin:
                    divide(f, q, 0)
                if nxt:
                    g_low(n, q, 3)
                if fin:
                    divide(f, q, 1)
                weights_high(s, it, p)
                if nxt:
                    for h in range(4):
                        maxima(n, h)
                if fin:
                    residual(f, q, it if p == 1 else it - 1)
                if p == 0 and late:
                    token_stats(it - 1)
                if known(s + 2, B):
                    stats(s + 2, p, it + 2)
                if nxt:
                    maxima(n, 4)
                if p == 0 and late:
                    need(dve, bnt_done, it)
                if known(s + 2, B):
                    need(dve, bn_done, s + 3)
                if nxt:
                    maxima(n, 5)
                if p == 0 and late:
                    token_aggregate()
                if known(s + 2, B):
                    aggregate(s + 2, p)
                if nxt:
                    for h in range(6, 8):
                        maxima(n, h)
                if p == 1 and late:
                    logits_out(it - 1)
                if nxt:
                    max_in(n, q)

            def finish():
                recip(B - 1)
                divide(B - 1, 1, 0)
                divide(B - 1, 1, 1)
                residual(B - 1, 1, PAIRS - 1)
                token_stats(PAIRS - 1)
                need(dve, bnt_done, PAIRS)
                token_aggregate()
                token_norm(PAIRS - 1)
                logits_out(PAIRS - 1)

            body_loop(dve, step, finish)

        @block.gpsimd
        def _(pool):
            pool.memset(minus_half[:, :], -0.5).then_inc(zero_done, 1)
            pool.memset(eps[:, :], EPS).then_inc(zero_done, 1)
            pool.memset(zero[:, :], 0.0).then_inc(zero_done, 1)

            def rstd_of(b, q):
                need(pool, stats_done, b + 1)
                need(pool, xn_done, b - 1)
                pool.tensor_tensor(ve[q][:, :], mv[q][:, 1:2], eps[:, :], ALU.add).then_inc(ve_done, 1)
                need(pool, ve_done, b + 1)
                pool.tensor_tensor(rstd[q][:, :], ve[q][:, :], minus_half[:, :], ALU.pow).then_inc(rstd_done, 1)

            def split_context(b, q, i):
                need(pool, c_in[q], 32 * i)
                need(pool, ring_filled, RN * (b - 2) + RING.index("U1") + 1)
                pool.tensor_tensor(ch[q][:, :], raw_c[q][:, :], zero[:, :].broadcast_to([P, N]), ALU.add).then_inc(ch_done, 1)
                need(pool, ch_done, b + 1)
                pool.tensor_tensor(cl[q][:, :], raw_c[q][:, :], ch[q][:, :].bitcast(F32), ALU.subtract).then_inc(cl_done, 1)

            def x_low(b, q):
                need(pool, xn_done, b + 1)
                need(pool, st_done, 8 * (b - 1))
                pool.tensor_tensor(xlm[q][0:C, :], xn[:, :], xh[q][0:C, :].bitcast(F32), ALU.subtract).then_inc(xl_done, 1)

            pool.wait_ge(zero_done, 6)
            split_context(0, 0, 1)
            rstd_of(0, 0)
            rstd_of(1, 1)
            x_low(0, 0)
            split_context(1, 1, 1)
            pool.wait_ge(tg_done, 1)

            def rz_low(f):
                need(pool, rzh_done, f + 1)
                pool.tensor_tensor(rzl[:, :], rz[:, :], rzh[:, :].bitcast(F32), ALU.subtract).then_inc(rzl_done, 1)

            def add_heads(f, fp):
                need(pool, mul_done, 2 * f + 2)
                o = os_[fp]
                pool.tensor_tensor(o[:, 0:2, :].rearrange("p k i -> p (k i)"), o[:, 0:2, :].rearrange("p k i -> p (k i)"),
                                   o[:, 2:4, :].rearrange("p k i -> p (k i)"), ALU.add).then_inc(add_done, 1)
                need(pool, add_done, f + 1)
                need(pool, y_done, f)
                pool.tensor_tensor(acc[:, :], o[:, 0, :], o[:, 1, :], ALU.add).then_inc(sum_done, 1)

            def weights_low(s, p):
                cols = bass.ds(s * W_STEP, W_STEP)
                need(pool, wh_done, s + 1)
                pool.tensor_tensor(w_lo[:, cols], w_raw[p][:, :], w_hi[:, cols].bitcast(F32), ALU.subtract).then_inc(wl_done, 1)

            def residual_x(it):
                need(pool, xr_in, 16 * (it + 1))
                pool.tensor_tensor(xr[:, :], xr[:, :], tgb[:, :].broadcast_to([P, N]), ALU.add).then_inc(xr_done, 1)

            def token_rstd(pair):
                need(pool, statt_done, pair + 1)
                pool.tensor_tensor(vet[:, :], mvt[:, 1:2], eps[:, :], ALU.add).then_inc(vet_done, 1)
                need(pool, vet_done, pair + 1)
                need(pool, xn2_done, pair)
                pool.tensor_tensor(rstdt[:, :], vet[:, :], minus_half[:, :], ALU.pow).then_inc(rstdt_done, 1)

            def token_low(pair):
                cols = bass.ds(P * pair, P)
                need(pool, xth_done, pair + 1)
                pool.tensor_tensor(xtl[:, :, cols], xt[:, :, :], xth[:, :, cols].bitcast(F32), ALU.subtract).then_inc(xtl_done, 1)

            def step(it, p):
                s, q = 2 * it + p, 1 - p
                n, f = s + 1, s - 1
                fin = not isinstance(s, int) or s > 0
                late = not isinstance(it, int) or it > 0
                if known(n, B):
                    x_low(n, q)
                if p == 1:
                    residual_x(it)
                if fin:
                    rz_low(f)
                    add_heads(f, q)
                weights_low(s, p)
                if known(s + 2, B):
                    split_context(s + 2, p, it + 2)
                if p == 0 and late:
                    token_rstd(it - 1)
                if known(s + 2, B):
                    rstd_of(s + 2, p)
                if p == 1 and late:
                    token_low(it - 1)

            def finish():
                rz_low(B - 1)
                add_heads(B - 1, 1)
                token_rstd(PAIRS - 1)
                token_low(PAIRS - 1)

            body_loop(pool, step, finish)

        attention.close()

        experts = stack.enter_context(ExitStack())

        def ffn_sb(name, shape, dt=F32):
            return experts.enter_context(nc.sbuf_tensor(name, shape, dt))

        top = ffn_sb("top", [P, PAIRS])
        score = ffn_sb("score", [P, PAIRS, E_ROUTED])
        left = ffn_sb("left", [P, PAIRS, E_ROUTED])
        hit = ffn_sb("hit", [P, PAIRS, E_ROUTED])
        pick = [ffn_sb(f"pick{t}", [P, PAIRS, E_ROUTED]) for t in range(2)]
        th = [ffn_sb(f"th{q}", [P, CHUNK]) for q in range(2)]
        hs = [ffn_sb(f"hs{q}", [P, CHUNK]) for q in range(2)]
        g = [ffn_sb(f"g{r}", [P, CHUNK]) for r in range(3)]
        gh = [ffn_sb(f"gh{r}", [P, CHUNK], F32R) for r in range(3)]
        gl = [ffn_sb(f"gl{r}", [P, CHUNK], F32R) for r in range(3)]


        UNITS = 2 * EXPERTS
        LAG = 2
        block = stack.enter_context(nc.Block())
        w1_of = lambda w, e, m, db: w[:, ((e * 2 + m) * DB + db) * INTER:((e * 2 + m) * DB + db + 1) * INTER]
        w2_of = lambda w, e: w[:, EXPERTS * 2 * DB * INTER + e * D:EXPERTS * 2 * DB * INTER + (e + 1) * D]
        y_banks = [(po[0], po[1]), (pz, pm)]

        @block.sync
        def _(sp):
            o_rows = out.rearrange("b c n -> (b c) n")
            with sp.Fori(0, CHUNKS // 2) as it:
                for half in range(2):
                    sp.wait_ge(y2_done, 2 * (UNITS * it + EXPERTS * (half + 1)))
                    for t in range(TILES):
                        tile = (2 * it + half) * TILES + t
                        sp.dma_start(o_rows[bass.ds(tile * P, P), :], x1[:, bass.ds(tile, 1), :].rearrange("p o d -> p (o d)")).then_inc(out_done, 16)
            sp.wait_ge(out_done, 16 * PAIRS)

        @block.tensor
        def _(pe):
            pe.wait_ge(wl_done, B)
            pe.wait_ge(xtl_done, PAIRS)
            with pe.Fori(0, CHUNKS // 2) as it:
                for j in range(UNITS + LAG):
                    if j < UNITS:
                        k, e = UNITS * it + j, j % EXPERTS
                        cols = bass.ds((2 * it + j // EXPERTS) * CHUNK, CHUNK)
                        if j < 2:
                            pe.wait_ge(g_done, k)
                        else:
                            pe.wait_ge(g_done, k - 1)
                        for m, bank_ in enumerate((ps[j % 2], pt[j % 2])):
                            for db in range(DB):
                                pe.matmul(bank_[:, :], w1_of(w_hi, e, m, db), xth[:, db, cols], start=(db == 0), stop=False)
                                pe.matmul(bank_[:, :], w1_of(w_hi, e, m, db), xtl[:, db, cols], start=False, stop=False)
                                mm = pe.matmul(bank_[:, :], w1_of(w_lo, e, m, db), xth[:, db, cols], start=False, stop=(db == DB - 1))
                        mm.then_inc(hu_filled, 1)
                    if j >= LAG:
                        k, i = UNITS * it + j - LAG, j - LAG
                        e, r = i % EXPERTS, i % 3
                        pe.wait_ge(glo_done, k + 1)
                        for half in range(2):
                            bank_ = y_banks[i % 2][half]
                            if i >= 2:
                                pe.wait_ge(y2_done, 2 * (k - 2) + half + 1)
                            for t in range(2):
                                o = bank_[:, D * t:D * t + D]
                                rows = slice(P * (2 * half + t), P * (2 * half + t) + P)
                                pe.matmul(o, gh[r][:, rows], w2_of(w_hi, e), start=True, stop=False)
                                pe.matmul(o, gh[r][:, rows], w2_of(w_lo, e), start=False, stop=False)
                                mm = pe.matmul(o, gl[r][:, rows], w2_of(w_hi, e), start=False, stop=True)
                            mm.then_inc(y2_filled, 1)
                pe.wait_ge(y2_done, 2 * UNITS * (it + 1))

        @block.scalar
        def _(act):
            act.wait_ge(rt_done, 2)
            act.activation(score[:, :, :], left[:, :, :], ACT.Exp).then_inc(rexp_done, 1)
            with act.Fori(0, CHUNKS // 2) as it:
                for j in range(UNITS + 1):
                    if j < UNITS:
                        k = UNITS * it + j
                        act.wait_ge(hu_filled, k + 1)
                        if j >= 2:
                            act.wait_ge(hs_done, k - 1)
                        act.activation(th[j % 2][:, :], ps[j % 2][:, :], ACT.Tanh, scale=0.5).then_inc(th_done, 1)
                    if j >= 1:
                        k, r = UNITS * it + j - 1, (j - 1) % 3
                        act.wait_ge(g_done, k + 1)
                        if j - 1 >= 3:
                            act.wait_ge(y2_filled, 2 * (k - 2))
                        act.activation(gh[r][:, :], g[r][:, :], ACT.Copy).then_inc(ghi_done, 1)

        @block.vector
        def _(dve):
            n = [0]

            def small(ins):
                ins.then_inc(rt_done, 1)
                n[0] += 1
                dve.wait_ge(rt_done, n[0])

            wide = lambda t: t[:, :].unsqueeze(2).broadcast_to([P, PAIRS, E_ROUTED])
            rank = kst[:, K_RANK:K_RANK + E_ROUTED].unsqueeze(1).broadcast_to([P, PAIRS, E_ROUTED])
            small(dve.tensor_reduce(top[:, :], logit[:, :, :], AX.X, ALU.max))
            small(dve.tensor_tensor(left[:, :, :], logit[:, :, :], wide(top), ALU.subtract))
            dve.wait_ge(rexp_done, 1)
            small(dve.tensor_reduce(top[:, :], score[:, :, :], AX.X, ALU.add))
            small(dve.reciprocal(top[:, :], top[:, :]))
            small(dve.tensor_tensor(score[:, :, :], score[:, :, :], wide(top), ALU.mult))
            src = score
            for t in range(2):
                small(dve.tensor_reduce(top[:, :], src[:, :, :], AX.X, ALU.max))
                small(dve.tensor_tensor(hit[:, :, :], src[:, :, :], wide(top), ALU.is_equal))
                small(dve.tensor_tensor(hit[:, :, :], hit[:, :, :], rank, ALU.mult))
                small(dve.tensor_reduce(top[:, :], hit[:, :, :], AX.X, ALU.max))
                small(dve.tensor_tensor(pick[t][:, :, :], hit[:, :, :], wide(top), ALU.is_equal))
                if t == 0:
                    small(dve.scalar_tensor_tensor(out=left[:, :, :], in0=pick[0][:, :, :], scalar=-2.0, in1=score[:, :, :], op0=ALU.mult, op1=ALU.add))
                    src = left
            small(dve.tensor_tensor(hit[:, :, :], pick[0][:, :, :], pick[1][:, :, :], ALU.add))
            small(dve.scalar_tensor_tensor(out=comb[:, :, 0:E_ROUTED], in0=hit[:, :, :], scalar=hgf[:, 0:1], in1=score[:, :, :], op0=ALU.mult, op1=ALU.mult))
            small(dve.tensor_scalar(comb[:, :, E_ROUTED], top[:, :], 0.0, hgf[:, 0:1], ALU.mult, ALU.add))

            with dve.Fori(0, CHUNKS // 2) as it:
                for j in range(UNITS + LAG + 1):
                    if j < UNITS:
                        k, q, r = UNITS * it + j, j % 2, j % 3
                        dve.wait_ge(th_done, k + 1)
                        dve.scalar_tensor_tensor(out=hs[q][:, :], in0=th[q][:, :], scalar=1.0, in1=ps[q][:, :], op0=ALU.add, op1=ALU.mult).then_inc(hs_done, 1)
                        dve.wait_ge(hs_done, k + 1)
                        if j >= 3:
                            dve.wait_ge(glo_done, k - 2)
                        dve.tensor_tensor(g[r][:, :], hs[q][:, :], pt[q][:, :], ALU.mult).then_inc(g_done, 1)
                    if j >= LAG + 1:
                        i = j - LAG - 1
                        k, e = UNITS * it + i, i % EXPERTS
                        for half in range(2):
                            dve.wait_ge(y2_filled, 2 * k + half + 1)
                            if e > 0:
                                dve.wait_ge(y2_done, 2 * k + half - 1)
                            for t in range(2):
                                tile = (2 * it + i // EXPERTS) * TILES + 2 * half + t
                                row = x1[:, bass.ds(tile, 1), :].rearrange("p o d -> p (o d)")
                                mm = dve.scalar_tensor_tensor(out=row, in0=y_banks[i % 2][half][:, D * t:D * t + D],
                                                              scalar=comb[:, bass.ds(tile, 1), e], in1=row, op0=ALU.mult, op1=ALU.add)
                            mm.then_inc(y2_done, 1)

        @block.gpsimd
        def _(pool):
            with pool.Fori(0, CHUNKS // 2) as it:
                for j in range(UNITS):
                    k, r = UNITS * it + j, j % 3
                    pool.wait_ge(ghi_done, k + 1)
                    if j >= 3:
                        pool.wait_ge(y2_filled, 2 * (k - 2))
                    pool.tensor_tensor(gl[r][:, :], g[r][:, :], gh[r][:, :].bitcast(F32), ALU.subtract).then_inc(glo_done, 1)


def kernel(**inputs):
    from concourse import bacc
    from concourse.bass_utils import run_bass_kernel_spmd

    def get(name):
        return np.ascontiguousarray(inputs[name])

    w1 = np.concatenate([get("L0_ffn_w1"), get("L0_ffn_ws1")[None]])
    w3 = np.concatenate([get("L0_ffn_w3"), get("L0_ffn_ws3")[None]])
    w2 = np.concatenate([get("L0_ffn_w2"), get("L0_ffn_ws2")[None]])
    w13T = np.stack([w1, w3], axis=1).reshape(EXPERTS, 2, INTER, DB, P).transpose(4, 0, 1, 3, 2).reshape(P, -1)
    w2T = w2.transpose(2, 0, 1).reshape(INTER, -1)
    arrays = {
        "x": get("x"), "ctx_in": get("ctx_2048"), "g_xattn": get("g_xattn"), "g_ffn": get("g_ffn"),
        "wq": get("L0_xattn_Wq"), "wk": get("L0_xattn_Wkv")[:HEADS * DH], "wv": get("L0_xattn_Wkv")[HEADS * DH:],
        "woT": get("L0_xattn_Wout").T, "bout": get("L0_xattn_bout"), "gateT": get("L0_ffn_gate_w").T,
        "w_all": np.concatenate([w13T, w2T], axis=1), "consts": constants(),
    }
    arrays = {f"in_{k}": np.ascontiguousarray(a) for k, a in arrays.items()}
    nc = bacc.Bacc("TRN2", target_bir_lowering=False, num_devices=1)
    args = [nc.dram_tensor(k, a.shape, mybir.dt.from_np(a.dtype), kind="ExternalInput").ap() for k, a in arrays.items()]
    out = nc.dram_tensor("out", (B, C, N), F32, kind="ExternalOutput").ap()
    build(nc, *args, out)
    r = run_bass_kernel_spmd(nc, [arrays], core_ids=[0])
    return r.results[0]["out"]
```

```python
from contextlib import ExitStack

import numpy as np

import concourse.bass as bass
from concourse import mybir

F32 = mybir.dt.float32
F32R = mybir.dt.float32r
ALU = mybir.AluOpType
ACT = mybir.ActivationFunctionType
AX = mybir.AxisListType

P = 128
B, C, N = 32, 64, 256
HEADS, DH = 8, 64
E_ROUTED, INTER = 8, 128
EXPERTS = E_ROUTED + 1
D = N
PAIRS = B // 2
JB = N // P
DB = D // P
EPS = 1e-5
CHUNK = 512
TILES = CHUNK // P
CHUNKS = B * C // CHUNK
LAG = 2
EARLY = PAIRS - 2
W_COLS = 2 * DB * INTER + D

RING = ["G0", "G1", "S0", "G2", "S1", "G3", "S2", "S3", "S4", "S5", "S6", "S7"]
BANKS = 3
RN = len(RING)

K_ID, K_HEAD, K_FOLD, K_DEN, K_RANK, K_LOW, K_PAIR = 0, 128, 136, 200, 328, 336, 337
K_KEPT = K_PAIR
K_COLS = K_PAIR + HEADS * P


def constants():
    k = np.zeros((P, K_COLS), np.float32)
    k[:, K_ID:K_ID + P] = np.eye(P)
    for h in range(HEADS):
        k[C + h, K_HEAD + h] = 1
        for ib in range(JB):
            row = 32 * (h % 4) + 2 * (h // 4) + ib
            at = K_PAIR + P * (JB * (h // 2) + ib) + C * (h % 2)
            k[row, at:at + C] = k[row + 4, at:at + C] = 1
    k[:, K_FOLD:K_FOLD + C] = np.vstack([np.eye(C), np.eye(C)])
    for use in range(4):
        at = K_DEN + 32 * use
        k[:, at + use] = k[:, at + use + 4] = 1
        if use == 0:
            k[:, at + 8:at + 32] = 1
    for t in range(4):
        k[32 * t + 4:32 * t + 8, K_LOW] = -1
    k[:, K_RANK:K_RANK + E_ROUTED] = E_ROUTED - np.arange(E_ROUTED)
    return k


def need(eng, sem, value):
    if not isinstance(value, int) or value > 0:
        eng.wait_ge(sem, value)


def build(nc, x, ctx_in, g_xattn, g_ffn, wq, wk, wv, woT, bout, gateT, w_all, consts, out):
    with ExitStack() as stack:
        def sb(name, shape, dt=F32):
            return stack.enter_context(nc.sbuf_tensor(name, shape, dt))

        def bank(name):
            return stack.enter_context(nc.psum_tensor(name, [P, 512], F32))

        def sem(name):
            return stack.enter_context(nc.semaphore(name))

        kst = sb("kst", [P, K_KEPT])
        ident_r = sb("ident_r", [P, P], F32R)
        pair_r = sb("pair_r", [P, HEADS, P], F32R)
        mhl = sb("mhl", [P, HEADS, P], F32R)
        nhl = sb("nhl", [P, HEADS, C], F32R)
        gates = sb("gates", [P, 2])
        tg = sb("tg", [P, 2])
        bo = sb("bo", [P, 1])
        tgb = sb("tgb", [P, 1])
        hgf = sb("hgf", [P, 1])
        minus_half = sb("minus_half", [P, 1])
        eps = sb("eps", [P, 1])
        gate_t = sb("gate_t", [P, DB, E_ROUTED])
        w_raw = [sb(f"w_raw{q}", [P, W_COLS]) for q in range(2)]
        w_hi = [sb(f"w_hi{q}", [P, W_COLS], F32R) for q in range(2)]
        w_lo = [sb(f"w_lo{q}", [P, W_COLS], F32R) for q in range(2)]
        x1 = sb("x1", [P, PAIRS, D])
        bn6t = sb("bn6t", [P, 6])
        mvt = sb("mvt", [P, 2])
        vet = sb("vet", [P, 1])
        rstdt = sb("rstdt", [P, 1])
        xn2 = sb("xn2", [P, D])
        xt = sb("xt", [P, DB, P])
        xth = sb("xth", [P, DB, B * C], F32R)
        xtl = sb("xtl", [P, DB, B * C], F32R)
        logit = sb("logit", [P, PAIRS, E_ROUTED])
        top = sb("top", [P, PAIRS])
        score = sb("score", [P, PAIRS, E_ROUTED])
        left = sb("left", [P, PAIRS, E_ROUTED])
        hit = sb("hit", [P, PAIRS, E_ROUTED])
        pick = sb("pick", [P, PAIRS, E_ROUTED])
        comb = sb("comb", [P, PAIRS, EXPERTS])

        raw_x = [sb(f"raw_x{q}", [P, N]) for q in range(2)]
        raw_c = [sb(f"raw_c{q}", [P, N]) for q in range(2)]
        bn6 = [sb(f"bn6_{q}", [P, 6]) for q in range(2)]
        mv = [sb(f"mv{q}", [P, 2]) for q in range(2)]
        ve = [sb(f"ve{q}", [P, 1]) for q in range(2)]
        rstd = [sb(f"rstd{q}", [P, 1]) for q in range(2)]
        xn = sb("xn", [C, N])
        xh = [sb(f"xh{q}", [P, N], F32R) for q in range(2)]
        xlm = [sb(f"xlm{q}", [P, N], F32R) for q in range(2)]
        ch = [sb(f"ch{q}", [P, N], F32R) for q in range(2)]
        cl = [sb(f"cl{q}", [P, N], F32R) for q in range(2)]
        ghl = [sb(f"ghl{q}", [P, HEADS, N], F32R) for q in range(2)]
        ghs = [sb(f"ghs{q}", [P, HEADS, N], F32R) for q in range(2)]
        u = [sb(f"u{q}", [P, JB, HEADS, C]) for q in range(2)]
        nmax = sb("nmax", [P, JB, P], F32R)
        ex = [sb(f"ex{h}", [P, JB, N]) for h in range(HEADS)]
        wq2, wk2, wv2 = (ex[h].rearrange("p b (k c) -> p (b k) c", c=2 * C).rearrange("p k (r c) -> p k r c", r=2) for h in range(3))
        wo = ex[3][:, 0, :].rearrange("p (k c) -> p k c", c=C)
        k_pair = [ex[h].rearrange("p b i -> p (b i)") for h in (4, 5)]
        ez = [sb(f"ez{t}", [P, N]) for t in range(4)]
        os_ = [sb(f"os{q}", [P, HEADS // 2, N]) for q in range(2)]
        rz = sb("rz", [P, P])
        rzh = sb("rzh", [P, P], F32R)
        rzc = sb("rzc", [P, P], F32R)
        acc = [sb(f"acc{q}", [P, N]) for q in range(2)]
        xr = sb("xr", [P, N])
        ps = [bank(f"ps{t}") for t in range(BANKS)]
        pt = [bank("pt0"), bank("pt1")]
        po, pz, pm = bank("po"), bank("pz"), bank("pm")
        th, hs, g = ([ex[h].rearrange("p b i -> p (b i)") for h in hs_] for hs_ in ((0, 1), (2, 3), (4, 5, 6, 7)))
        gh, gl = ([t[:, JB * r:JB * r + 2, :].rearrange("p h j -> p (h j)") for r in range(4)] for t in (ghl[0], ghs[0]))
        y_banks = [(ps[2], po), (pz, pm)]

        setup_in = sem("setup_in")
        small_in = sem("small_in")
        w_in = [sem(f"w_in{q}") for q in range(2)]
        consts_done = sem("consts_done")
        zero_done = sem("zero_done")
        tanh_done = sem("tanh_done")
        tg_done = sem("tg_done")
        mprod_done = sem("mprod_done")
        mhi_done = sem("mhi_done")
        mhl_done = sem("mhl_done")
        x_in = [sem(f"x_in{q}") for q in range(2)]
        c_in = [sem(f"c_in{q}") for q in range(2)]
        xr_in = sem("xr_in")
        bn_done = sem("bn_done")
        stats_done = sem("stats_done")
        ve_done = sem("ve_done")
        rstd_done = sem("rstd_done")
        xh_done = sem("xh_done")
        xn_done = sem("xn_done")
        xl_done = sem("xl_done")
        ch_done = sem("ch_done")
        cl_done = sem("cl_done")
        ring_filled = sem("ring_filled")
        u_filled = sem("u_filled")
        gh_done = sem("gh_done")
        gs_done = sem("gs_done")
        gl_done = sem("gl_done")
        u_done = sem("u_done")
        max_done = sem("max_done")
        mt_filled = sem("mt_filled")
        mt_done = sem("mt_done")
        st_done = sem("st_done")
        exp_done = sem("exp_done")
        av_done = sem("av_done")
        z_done = sem("z_done")
        os_done = sem("os_done")
        recip_done = sem("recip_done")
        rzh_done = sem("rzh_done")
        rzc_done = sem("rzc_done")
        ez_done = sem("ez_done")
        rb_done = sem("rb_done")
        mul_done = sem("mul_done")
        add_done = sem("add_done")
        sum_done = sem("sum_done")
        y_done = sem("y_done")
        xr_done = sem("xr_done")
        res_done = sem("res_done")
        bnt_done = sem("bnt_done")
        statt_done = sem("statt_done")
        vet_done = sem("vet_done")
        rstdt_done = sem("rstdt_done")
        xn2_done = sem("xn2_done")
        tr_done = sem("tr_done")
        xt_done = sem("xt_done")
        xth_done = sem("xth_done")
        xtl_done = sem("xtl_done")
        lg_filled = sem("lg_filled")
        logits_free = sem("logits_free")
        wh_done = sem("wh_done")
        wl_done = sem("wl_done")
        rt_done = sem("rt_done")
        left_done = sem("left_done")
        rexp_done = sem("rexp_done")
        hu_filled = sem("hu_filled")
        th_done = sem("th_done")
        hs_done = sem("hs_done")
        g_done = sem("g_done")
        ghi_done = sem("ghi_done")
        glo_done = sem("glo_done")
        y2_filled = sem("y2_filled")
        y2_done = sem("y2_done")
        out_done = sem("out_done")

        def body_loop(eng, step, finish):
            step(0, 0)
            step(0, 1)
            with eng.Fori(1, PAIRS - 1) as it:
                step(it, 0)
                step(it, 1)
            step(PAIRS - 1, 0)
            step(PAIRS - 1, 1)
            finish()

        def known(v, limit):
            return not isinstance(v, int) or v < limit

        def w1_of(w, m, db):
            return w[:, (m * DB + db) * INTER:(m * DB + db + 1) * INTER]

        def w2_of(w):
            return w[:, 2 * DB * INTER:]

        def expert_loop(eng, unit):
            steps = (EXPERTS - 1) // 2
            with eng.Fori(0, steps - 1) as it:
                for j in range(2 * CHUNKS):
                    unit(CHUNKS + 2 * CHUNKS * it + j, j, it)
            for j in range(2 * CHUNKS):
                unit(CHUNKS + 2 * CHUNKS * (steps - 1) + j, j, steps - 1)

        block = stack.enter_context(nc.Block())

        @block.sync
        def _(sp):
            def load(b, q, b_after):
                need(sp, xn_done, b_after)
                for r in (0, C):
                    sp.dma_start(raw_x[q][r:r + C, :], x[bass.ds(b, 1), :, :].rearrange("o c n -> (o c) n")).then_inc(x_in[q], 16)
                need(sp, cl_done, b_after)
                for r in (0, C):
                    sp.dma_start(raw_c[q][r:r + C, :], ctx_in[bass.ds(b, 1), :, :].rearrange("o c n -> (o c) n")).then_inc(c_in[q], 16)

            for t, w in ((wq2, wq), (wk2, wk), (wv2, wv)):
                for r in range(2):
                    sp.dma_start(t[:, :, r, :], w.rearrange("(k p) c -> p k c", p=P)).then_inc(setup_in, 16)
            sp.dma_start(wo[:, :, :], woT.rearrange("(k p) c -> p k c", p=P)).then_inc(setup_in, 16)
            sp.dma_start(kst[:, :], consts[:, 0:K_KEPT]).then_inc(setup_in, 16)
            for t in range(2):
                sp.dma_start(k_pair[t], consts[:, K_PAIR + 512 * t:K_PAIR + 512 * t + 512]).then_inc(setup_in, 16)
            load(0, 0, 0)
            load(1, 1, 0)
            for t, g in enumerate((g_xattn, g_ffn)):
                sp.dma_start(gates[:, t:t + 1], g.rearrange("(a o) -> a o", a=1).broadcast_to([P, 1])).then_inc(small_in, 16)
            for r in (0, C):
                sp.dma_start(bo[r:r + C, :], bout.rearrange("(c o) -> c o", o=1)).then_inc(small_in, 16)
            sp.dma_start(gate_t[:, :, :], gateT.rearrange("(k p) e -> p k e", p=P)).then_inc(small_in, 16)

            def weights(e, q):
                need(sp, wl_done, e - 1)
                sp.dma_start(w_raw[q][:, :], w_all[bass.ds(e, 1), :, :].rearrange("o p w -> (o p) w")).then_inc(w_in[q], 16)

            weights(0, 0)
            weights(1, 1)

            def step(it, p):
                s = 2 * it + p
                if known(s + 2, B):
                    load(s + 2, p, s + 1)
                if p == 1:
                    need(sp, res_done, it)
                    sp.dma_start(xr[:, :], x[bass.ds(2 * it, 2), :, :].rearrange("b c n -> (b c) n")).then_inc(xr_in, 16)

            def finish():
                with sp.Fori(1, EXPERTS // 2) as i:
                    weights(2 * i, 0)
                    weights(2 * i + 1, 1)
                weights(EXPERTS - 1, 0)
                o_rows = out.rearrange("(t b) c n -> (b c) t n", b=2)
                last = CHUNKS * (EXPERTS - 1)
                for c in range(CHUNKS):
                    for half in range(2):
                        sp.wait_ge(y2_done, 2 * (last + c) + half + 1)
                        tiles = slice(TILES * c + 2 * half, TILES * c + 2 * half + 2)
                        sp.dma_start(o_rows[:, tiles, :], x1[:, tiles, :]).then_inc(out_done, 16)
                sp.wait_ge(out_done, 16 * 2 * CHUNKS)

            body_loop(sp, step, finish)

        @block.tensor
        def _(pe):
            pe.wait_ge(setup_in, 16 * 10)
            for h in range(HEADS):
                r, k = DH * (h % 2), h // 2
                pe.matmul(ps[h % 2][:, P * k:P * k + P], wk2[r:r + DH, k, :, :].rearrange("d r c -> d (r c)"),
                          wq2[r:r + DH, k, :, :].rearrange("d r c -> d (r c)"), start=True, stop=True)
            for h in range(HEADS):
                r, k = DH * (h % 2), h // 2
                mm = pe.matmul(pt[h % 2][:, C * k:C * k + C], wv2[r:r + DH, k, :, :].rearrange("d r c -> d (r c)"),
                               wo[r:r + DH, k, :], start=True, stop=True)
            mm.then_inc(mprod_done, 1)
            pe.wait_ge(mhl_done, 4)
            pe.wait_ge(consts_done, 4)
            pe.wait_ge(zero_done, 5)

            def ring(use, b, q):
                k = RING.index(use)
                bank_ = ps[k % BANKS]
                before, back = RING[(k - BANKS) % RN], b if k >= BANKS else b - 1
                i = int(before[1])
                if before[0] == "G":
                    need(pe, gl_done, 4 * back + i + 1)
                    need(pe, gs_done, 4 * back + i + 1)
                else:
                    need(pe, max_done, 8 * back + i + 1)
                i = int(use[1])
                if use[0] == "G":
                    need(pe, cl_done, b + 1)
                    for h in range(2):
                        pe.matmul(bank_[:, N * h:N * h + N], mhl[:, 2 * i + h, :], ch[q][:, :], start=True, stop=False)
                        mm = pe.matmul(bank_[:, N * h:N * h + N], mhl[:, 2 * i + h, :], cl[q][:, :], start=False, stop=True)
                else:
                    need(pe, gl_done, 4 * b + i // 2 + 1)
                    need(pe, xh_done, b + 1)
                    for ib in range(JB):
                        mm = pe.matmul(bank_[:, N * ib:N * ib + N], xh[q][:, P * ib:P * ib + P], ghl[q][:, i, :], start=True, stop=True)
                mm.then_inc(ring_filled, 1)

            def values(b, q, i, free_sem, free_at):
                need(pe, cl_done, b + 1)
                need(pe, free_sem, free_at)
                js = slice(P * i, P * i + P)
                pe.matmul(po[:, :], ch[q][:, js], nhl[:, :, :].rearrange("p h c -> p (h c)"), start=True, stop=False)
                pe.matmul(po[:, :], cl[q][:, js], nhl[:, :, :].rearrange("p h c -> p (h c)"), start=False, stop=True).then_inc(u_filled, 1)

            def max_rows(b, free_sem, free_at):
                need(pe, max_done, 8 * b + 8)
                need(pe, free_sem, free_at)
                for ib in range(JB):
                    mm = pe.matmul(pm[:, P * ib:P * ib + P], nmax[:, ib, :], ident_r[:, :], start=True, stop=True)
                mm.then_inc(mt_filled, 1)

            def scores(s, p, h):
                if h == 0:
                    need(pe, xl_done, s + 1)
                    need(pe, mt_done, s + 1)
                    need(pe, gs_done, 4 * s + 4)
                need(pe, exp_done, 8 * s + h - 1)
                for jb in range(JB):
                    js = slice(P * jb, P * jb + P)
                    pe.matmul(pt[h % 2][:, N * jb:N * jb + N], ghl[p][:, h, js], xh[p][:, :], start=True, stop=False)
                    mm = pe.matmul(pt[h % 2][:, N * jb:N * jb + N], ghs[p][:, h, js], xlm[p][:, :], start=False, stop=True)
                mm.then_inc(st_done, 1)

            def weighted(s, p, k, free_sem, free_at):
                need(pe, exp_done, 8 * s + 2 * k + 2)
                need(pe, u_done, 2 * s + 2)
                need(pe, free_sem, free_at)
                for jb in range(JB):
                    for r in range(2):
                        h = 2 * k + r
                        mm = pe.matmul(po[C * r:C * r + C, 0:N], u[p][:, jb, h, :], ex[h][:, jb, :],
                                       start=(jb == 0), stop=(jb == JB - 1))
                mm.then_inc(av_done, 1)

            def denominators(s, k):
                need(pe, ez_done, 8 * s + 4 * k + 4)
                if k == 0:
                    need(pe, recip_done, 2 * s)
                for ib in range(JB):
                    for t in range(4):
                        at = K_DEN + 32 * (2 * k + ib)
                        mm = pe.matmul(pz[32 * t:32 * t + 32, 0:P], kst[:, at:at + 32], ez[t][:, P * ib:P * ib + P],
                                       start=(k == 0 and ib == 0), stop=(k == 1 and ib == JB - 1))
                mm.then_inc(z_done, 1)

            def spread(f, k, free_sem, free_at):
                need(pe, rzc_done, f + 1)
                need(pe, free_sem, free_at)
                for r in range(2 * JB):
                    mm = pe.matmul(pm[:, P * r:P * r + P], pair_r[:, 2 * JB * k + r, :], rzc[:, :], start=True, stop=True)
                mm.then_inc(rb_done, 1)

            def fold(pair, free_sem, free_at):
                need(pe, sum_done, 2 * pair + 2)
                need(pe, free_sem, free_at)
                for r in range(2):
                    mm = pe.matmul(pm[C * r:C * r + C, 0:N], kst[:, K_FOLD:K_FOLD + C], acc[r][:, :], start=True, stop=True)
                mm.then_inc(y_done, 1)

            def turn(pair, free_sem, free_at):
                need(pe, xn2_done, pair + 1)
                need(pe, free_sem, free_at)
                for db in range(DB):
                    mm = pe.transpose(po[:, P * db:P * db + P], xn2[:, P * db:P * db + P], kst[:, K_ID:K_ID + P])
                mm.then_inc(tr_done, 1)

            def route(pair):
                need(pe, xt_done, pair + 1)
                for db in range(DB):
                    mm = pe.matmul(po[:, 0:E_ROUTED], xt[:, db, :], gate_t[:, db, :], start=(db == 0), stop=(db == DB - 1))
                mm.then_inc(lg_filled, 1)

            for use in RING:
                ring(use, 0, 0)
            values(0, 0, 0, mhl_done, 0)
            values(0, 0, 1, u_done, 1)
            ring("G0", 1, 1)
            ring("G1", 1, 1)
            max_rows(0, mhl_done, 0)

            def step(it, p):
                s, q = 2 * it + p, 1 - p
                n, f = s + 1, s - 1
                nxt = known(n, B)
                fin = not isinstance(s, int) or s > 0
                tok = p == 1 and (not isinstance(it, int) or it > 0)

                def r(*uses):
                    if nxt:
                        for use in uses:
                            ring(use, n, q)

                if fin:
                    if p == 0:
                        pe.wait_ge(logits_free, it)
                    weighted(f, q, 2, os_done, 4 * f + 2)
                r("S0")
                scores(s, p, 0)
                r("G2")
                if fin:
                    weighted(f, q, 3, os_done, 4 * f + 3)
                if tok:
                    fold(it - 1, mt_done, s + 1)
                scores(s, p, 1)
                if fin:
                    denominators(f, 1)
                r("S1", "G3")
                if nxt:
                    values(n, q, 0, *((os_done, 4 * s) if fin else (u_done, 2)))
                scores(s, p, 2)
                r("S2")
                scores(s, p, 3)
                r("S3")
                weighted(s, p, 0, *((u_done, 2 * n + 1) if nxt else (os_done, 4 * s)))
                scores(s, p, 4)
                r("S4")
                if nxt:
                    values(n, q, 1, os_done, 4 * s + 1)
                if fin:
                    spread(f, 0, *((res_done, it) if tok else (mt_done, s + 1)))
                scores(s, p, 5)
                r("S5")
                weighted(s, p, 1, *((u_done, 2 * n + 2) if nxt else (os_done, 4 * s + 1)))
                denominators(s, 0)
                r("S6")
                if fin:
                    spread(f, 1, mul_done, 2 * f + 1)
                r("S7")
                scores(s, p, 6)
                if tok:
                    turn(it - 1, os_done, 4 * s + 2)
                scores(s, p, 7)
                if known(s + 2, B):
                    ring("G0", s + 2, p)
                if tok:
                    route(it - 1)
                if known(s + 2, B):
                    ring("G1", s + 2, p)
                if nxt:
                    max_rows(n, mul_done, 2 * f + 2)

            def first(k, j, e, q):
                c = j % CHUNKS
                if isinstance(e, int) and e == 0:
                    pe.wait_ge(xtl_done, TILES * (c + 1))
                if c == 0:
                    pe.wait_ge(wl_done, e + 1)
                need(pe, g_done, k - 1)
                cols = slice(CHUNK * c, CHUNK * (c + 1))
                for m, bank_ in enumerate((ps[j % 2], pt[j % 2])):
                    for db in range(DB):
                        pe.matmul(bank_[:, :], w1_of(w_hi[q], m, db), xth[:, db, cols], start=(db == 0), stop=False)
                        pe.matmul(bank_[:, :], w1_of(w_hi[q], m, db), xtl[:, db, cols], start=False, stop=False)
                        mm = pe.matmul(bank_[:, :], w1_of(w_lo[q], m, db), xth[:, db, cols], start=False, stop=(db == DB - 1))
                mm.then_inc(hu_filled, 1)

            def second(k, j, q):
                r = j % 4
                pe.wait_ge(glo_done, k + 1)
                for half in range(2):
                    bank_ = y_banks[j % 2][half]
                    need(pe, y2_done, 2 * (k - LAG) + half + 1)
                    for t in range(2):
                        o = bank_[:, D * t:D * t + D]
                        rows = slice(P * (2 * half + t), P * (2 * half + t) + P)
                        pe.matmul(o, gh[r][:, rows], w2_of(w_hi[q]), start=True, stop=False)
                        pe.matmul(o, gh[r][:, rows], w2_of(w_lo[q]), start=False, stop=False)
                        mm = pe.matmul(o, gl[r][:, rows], w2_of(w_hi[q]), start=False, stop=True)
                    mm.then_inc(y2_filled, 1)

            def finish():
                pe.wait_ge(logits_free, PAIRS)
                weighted(B - 1, 1, 2, os_done, 4 * B - 2)
                weighted(B - 1, 1, 3, os_done, 4 * B - 1)
                denominators(B - 1, 1)
                first(0, 0, 0, 0)
                spread(B - 1, 0, mul_done, 2 * B - 2)
                spread(B - 1, 1, mul_done, 2 * B - 1)
                first(1, 1, 0, 0)
                fold(PAIRS - 1, mul_done, 2 * B)
                first(2, 2, 0, 0)
                turn(PAIRS - 1, os_done, 4 * B)
                route(PAIRS - 1)
                pe.wait_ge(logits_free, PAIRS + 1)
                second(0, 0, 0)
                pe.wait_ge(res_done, PAIRS)
                second(1, 1, 0)
                first(3, 3, 0, 0)

                def unit(k, j, step):
                    first(k, j, 1 + 2 * step + j // CHUNKS, (1 + j // CHUNKS) % 2)
                    second(k - LAG, j + LAG, (j + LAG) // CHUNKS % 2)

                expert_loop(pe, unit)
                for k in range(CHUNKS * EXPERTS - LAG, CHUNKS * EXPERTS):
                    second(k, k, 0)

            body_loop(pe, step, finish)

        @block.scalar
        def _(act):
            def g_high(b, q, i):
                need(act, ring_filled, RN * b + RING.index(f"G{i}") + 1)
                src = ps[RING.index(f"G{i}") % BANKS]
                act.activation(ghl[q][:, 2 * i:2 * i + 2, :].rearrange("p h j -> p (h j)"), src[:, :], ACT.Copy).then_inc(gh_done, 1)

            def g_again(b, q, i):
                need(act, ring_filled, RN * b + RING.index(f"G{i}") + 1)
                src = ps[RING.index(f"G{i}") % BANKS]
                act.activation(ghs[q][0:C, 2 * i:2 * i + 2, :].rearrange("p h j -> p (h j)"), src[0:C, :], ACT.Copy).then_inc(gs_done, 1)

            def u_out(b, q, i):
                need(act, u_filled, 2 * b + i + 1)
                act.activation(u[q][:, i, :, :].rearrange("p h c -> p (h c)"), po[:, :], ACT.Copy).then_inc(u_done, 1)

            def max_in(b, q):
                need(act, mt_filled, b + 1)
                act.activation(xlm[q][C:C + HEADS, :], pm[C:C + HEADS, 0:N], ACT.Copy).then_inc(mt_done, 1)

            def context_high(b, q, i):
                need(act, c_in[q], 32 * i)
                need(act, u_filled, 2 * (b - 1))
                act.activation(ch[q][:, :], raw_c[q][:, :], ACT.Copy).then_inc(ch_done, 1)

            def weights_high(e, q, i):
                need(act, w_in[q], 16 * i)
                need(act, y2_filled, 2 * CHUNKS * (e - 1))
                act.activation(w_hi[q][:, :], w_raw[q][:, :], ACT.Copy).then_inc(wh_done, 1)

            def expo(s, h):
                need(act, st_done, 8 * s + h + 1)
                need(act, av_done, 4 * (s - 1) + h // 2 + 1)
                need(act, ez_done, 8 * (s - 1) + h + 1)
                act.activation(ex[h][:, :, :].rearrange("p b i -> p (b i)"), pt[h % 2][:, :], ACT.Exp).then_inc(exp_done, 1)

            def sums_out(s, p, k):
                need(act, av_done, 4 * s + k + 1)
                if k == 0:
                    need(act, sum_done, s - 1)
                act.activation(os_[p][:, k, :], po[:, 0:N], ACT.Copy).then_inc(os_done, 1)

            def rz_high(f):
                need(act, recip_done, 2 * f + 2)
                need(act, rzc_done, f)
                act.activation(rzh[:, :], rz[:, :], ACT.Copy).then_inc(rzh_done, 1)

            def turned(pair):
                need(act, tr_done, pair + 1)
                need(act, lg_filled, pair)
                need(act, xtl_done, pair)
                act.activation(xt[:, :, :].rearrange("p b t -> p (b t)"), po[:, 0:D], ACT.Copy).then_inc(xt_done, 1)

            def turned_high(pair):
                need(act, xt_done, pair + 1)
                act.activation(xth[:, :, bass.ds(P * pair, P)], xt[:, :, :], ACT.Copy).then_inc(xth_done, 1)

            context_high(0, 0, 1)
            act.wait_ge(mprod_done, 1)
            for r in range(2):
                act.activation(mhl[:, r:HEADS:2, :], ps[r][:, :].rearrange("p (k c) -> p k c", c=P), ACT.Copy).then_inc(mhi_done, 1)
            for r in range(2):
                act.activation(nhl[:, r:HEADS:2, :], pt[r][:, 0:4 * C].rearrange("p (k c) -> p k c", c=C), ACT.Copy).then_inc(mhi_done, 1)
            act.wait_ge(small_in, 16 * 5)
            act.activation(tg[:, :], gates[:, :], ACT.Tanh).then_inc(tanh_done, 1)

            for use in RING:
                if use[0] == "G":
                    g_high(0, 0, int(use[1]))
                    g_again(0, 0, int(use[1]))
            u_out(0, 0, 0)
            u_out(0, 0, 1)
            context_high(1, 1, 1)
            g_high(1, 1, 0)
            g_high(1, 1, 1)
            max_in(0, 0)
            g_again(1, 1, 0)

            def step(it, p):
                s, q = 2 * it + p, 1 - p
                n, f = s + 1, s - 1
                nxt = known(n, B)
                fin = not isinstance(s, int) or s > 0
                tok = p == 1 and (not isinstance(it, int) or it > 0)

                if fin:
                    sums_out(f, q, 2)
                if nxt:
                    g_again(n, q, 1)
                expo(s, 0)
                if nxt:
                    g_high(n, q, 2)
                if fin:
                    sums_out(f, q, 3)
                expo(s, 1)
                if nxt:
                    g_again(n, q, 2)
                    g_high(n, q, 3)
                    u_out(n, q, 0)
                    g_again(n, q, 3)
                expo(s, 2)
                expo(s, 3)
                if fin:
                    rz_high(f)
                sums_out(s, p, 0)
                if known(s + 2, B):
                    context_high(s + 2, p, it + 2)
                expo(s, 4)
                if nxt:
                    u_out(n, q, 1)
                else:
                    router_exp(0, slice(0, EARLY))
                expo(s, 5)
                sums_out(s, p, 1)
                if not known(s + 2, B):
                    weights_high(p, p, 1)
                expo(s, 6)
                if tok:
                    turned(it - 1)
                expo(s, 7)
                if known(s + 2, B):
                    g_high(s + 2, p, 0)
                    g_high(s + 2, p, 1)
                if nxt:
                    max_in(n, q)
                if tok:
                    turned_high(it - 1)
                if known(s + 2, B):
                    g_again(s + 2, p, 0)

            def router_exp(part, pairs):
                act.wait_ge(left_done, part + 1)
                act.activation(score[:, pairs, :], left[:, pairs, :], ACT.Exp).then_inc(rexp_done, 1)

            def tanh_half(k, j):
                act.wait_ge(hu_filled, k + 1)
                need(act, hs_done, k - 1)
                act.activation(th[j % 2], ps[j % 2][:, :], ACT.Tanh, scale=0.5).then_inc(th_done, 1)

            def hidden_high(k, j):
                act.wait_ge(g_done, k + 1)
                need(act, y2_filled, 2 * (k - 3))
                act.activation(gh[j % 4], g[j % 4], ACT.Copy).then_inc(ghi_done, 1)

            def finish():
                sums_out(B - 1, 1, 2)
                sums_out(B - 1, 1, 3)
                rz_high(B - 1)
                tanh_half(0, 0)
                hidden_high(0, 0)
                tanh_half(1, 1)
                hidden_high(1, 1)
                tanh_half(2, 2)
                turned(PAIRS - 1)
                turned_high(PAIRS - 1)
                hidden_high(2, 2)
                router_exp(1, slice(EARLY, PAIRS))
                tanh_half(3, 3)
                hidden_high(3, 3)

                def unit(k, j, step):
                    e = 1 + 2 * step + j // CHUNKS
                    if j % CHUNKS == 2 and known(e + 1, EXPERTS):
                        weights_high(e + 1, j // CHUNKS, 2 + step)
                    tanh_half(k, j)
                    hidden_high(k, j)

                expert_loop(act, unit)

            body_loop(act, step, finish)

        @block.vector
        def _(dve):
            dve.memset(nmax[:, :, :].bitcast(F32), 0.0).then_inc(zero_done, 1)
            for q in range(2):
                dve.memset(xlm[q][C:P, :].bitcast(F32), 0.0).then_inc(zero_done, 1)
            dve.wait_ge(setup_in, 16 * 10)
            dve.tensor_scalar(ident_r[:, :], kst[:, K_ID:K_ID + P], 1.0, None, ALU.mult).then_inc(consts_done, 1)
            for t in range(2):
                dve.tensor_scalar(pair_r[:, 4 * t:4 * t + 4, :].rearrange("p k m -> p (k m)"), k_pair[t], 1.0, None, ALU.mult).then_inc(consts_done, 1)

            def stats(b, q, i):
                need(dve, x_in[q], 32 * i)
                dve.bn_stats(bn6[q][:, :], raw_x[q][:, :]).then_inc(bn_done, 1)

            def aggregate(b, q):
                dve.bn_aggr(mv[q][:, :], bn6[q][:, :]).then_inc(stats_done, 1)

            def norm_high(b, q):
                need(dve, rstd_done, b + 1)
                need(dve, st_done, 8 * (b - 1))
                dve.tensor_scalar(xh[q][:, :], raw_x[q][:, :], mv[q][:, 0:1], rstd[q][:, 0:1], ALU.subtract, ALU.mult).then_inc(xh_done, 1)

            def norm_full(b, q):
                need(dve, xl_done, b)
                dve.tensor_scalar(xn[:, :], raw_x[q][0:C, :], mv[q][0:C, 0:1], rstd[q][0:C, 0:1], ALU.subtract, ALU.mult).then_inc(xn_done, 1)

            for q in range(2):
                stats(q, q, 1)
                dve.wait_ge(bn_done, q + 1)
                aggregate(q, q)
            for q in range(2):
                sel = dve.tensor_copy(ghs[q][C:P, :, :], kst[C:P, K_HEAD:K_HEAD + HEADS].unsqueeze(2).broadcast_to([C, HEADS, N]))
            sel.then_inc(consts_done, 1)
            for t, (dst, src, w) in enumerate(((mhl, ps, P), (mhl, ps, P), (nhl, pt, C), (nhl, pt, C))):
                r = t % 2
                dve.wait_ge(mhi_done, t + 1)
                lo = dst[C:P, r:HEADS:2, :]
                dve.tensor_tensor(lo, src[r][C:P, 0:4 * w].rearrange("p (k c) -> p k c", c=w), lo.bitcast(F32), ALU.subtract).then_inc(mhl_done, 1)
            norm_high(0, 0)
            norm_full(0, 0)
            dve.wait_ge(tanh_done, 1)
            dve.tensor_tensor(tgb[:, :], tg[:, 0:1], bo[:, :], ALU.mult).then_inc(tg_done, 1)
            dve.tensor_scalar(hgf[:, :], tg[:, 1:2], 0.5, None, ALU.mult).then_inc(tg_done, 1)
            dve.wait_ge(tg_done, 2)
            dve.tensor_copy(comb[:, :, E_ROUTED], hgf[:, :].broadcast_to([P, PAIRS])).then_inc(logits_free, 1)

            def g_low(b, q, i):
                need(dve, gh_done, 4 * b + i + 1)
                lo = ghl[q][C:P, 2 * i:2 * i + 2, :].rearrange("p h j -> p (h j)")
                dve.tensor_tensor(lo, ps[RING.index(f"G{i}") % BANKS][C:P, :], lo.bitcast(F32), ALU.subtract).then_inc(gl_done, 1)

            def maxima(b, h):
                k = RING.index(f"S{h}")
                need(dve, ring_filled, RN * b + k + 1)
                dve.tensor_reduce(nmax[:, :, C + h], ps[k % BANKS][:, :].rearrange("p (b j) -> p b j", j=N), AX.X, ALU.max, negate=True).then_inc(max_done, 1)

            def recip(f, half):
                cols = slice(64 * half, 64 * half + 64)
                need(dve, z_done, 2 * f + 2)
                need(dve, rzc_done, f)
                dve.reciprocal(rz[:, cols], pz[:, cols]).then_inc(recip_done, 1)

            def rz_split(f):
                need(dve, rzh_done, f + 1)
                need(dve, rb_done, 2 * f)
                dve.scalar_tensor_tensor(out=rzc[:, :], in0=rzh[:, :].bitcast(F32), scalar=kst[:, K_LOW:K_LOW + 1], in1=rz[:, :],
                                         op0=ALU.mult, op1=ALU.add).then_inc(rzc_done, 1)

            def divide(f, fp, k):
                need(dve, rb_done, 2 * f + k + 1)
                need(dve, os_done, 4 * f + 2 * k + 2)
                o = os_[fp][:, 2 * k:2 * k + 2, :].rearrange("p k i -> p (k i)")
                dve.tensor_tensor(o, o, pm[:, :], ALU.mult).then_inc(mul_done, 1)

            def residual(pair):
                need(dve, y_done, pair + 1)
                need(dve, xr_done, pair + 1)
                dve.scalar_tensor_tensor(out=x1_of(pair), in0=pm[:, 0:N], scalar=tg[:, 0:1], in1=xr[:, :],
                                         op0=ALU.mult, op1=ALU.add).then_inc(res_done, 1)

            def x1_of(pair):
                return x1[:, bass.ds(pair, 1), :].rearrange("p o d -> p (o d)")

            def token_stats(pair):
                dve.bn_stats(bn6t[:, :], x1_of(pair)).then_inc(bnt_done, 1)

            def token_aggregate():
                dve.bn_aggr(mvt[:, :], bn6t[:, :]).then_inc(statt_done, 1)

            def token_norm(pair):
                need(dve, rstdt_done, pair + 1)
                need(dve, tr_done, pair)
                dve.tensor_scalar(xn2[:, :], x1_of(pair), mvt[:, 0:1], rstdt[:, 0:1], ALU.subtract, ALU.mult).then_inc(xn2_done, 1)

            def logits_out(pair):
                need(dve, lg_filled, pair + 1)
                dve.tensor_copy(logit[:, bass.ds(pair, 1), :].rearrange("p o e -> p (o e)"), po[:, 0:E_ROUTED]).then_inc(logits_free, 1)

            for use in RING:
                if use[0] == "G":
                    g_low(0, 0, int(use[1]))
                if use[0] == "S":
                    maxima(0, int(use[1]))
            norm_high(1, 1)
            g_low(1, 1, 0)
            g_low(1, 1, 1)
            norm_full(1, 1)

            def step(it, p):
                s, q = 2 * it + p, 1 - p
                n, f = s + 1, s - 1
                nxt = known(n, B)
                fin = not isinstance(s, int) or s > 0
                late = not isinstance(it, int) or it > 0
                tok = p == 1 and late

                def m(*hs):
                    if nxt:
                        for h in hs:
                            maxima(n, h)

                if not nxt:
                    router_start(slice(0, EARLY))
                m(0)
                if nxt:
                    g_low(n, q, 2)
                if known(s + 2, B):
                    stats(s + 2, p, it + 2)
                m(1)
                if fin:
                    recip(f, 0)
                if nxt:
                    g_low(n, q, 3)
                if fin:
                    recip(f, 1)
                if known(s + 2, B):
                    need(dve, bn_done, s + 3)
                if tok:
                    residual(it - 1)
                m(2)
                if known(s + 2, B):
                    aggregate(s + 2, p)
                if tok:
                    need(dve, res_done, it)
                if fin:
                    rz_split(f)
                if tok:
                    token_stats(it - 1)
                    need(dve, bnt_done, it)
                m(3)
                if tok:
                    token_aggregate()
                m(4)
                if fin:
                    divide(f, q, 0)
                m(5)
                if tok:
                    token_norm(it - 1)
                m(6)
                if fin:
                    divide(f, q, 1)
                m(7)
                if not nxt:
                    router_pick(0, slice(0, EARLY))
                if known(s + 2, B):
                    norm_high(s + 2, p)
                if tok:
                    logits_out(it - 1)
                if known(s + 2, B):
                    g_low(s + 2, p, 0)
                    g_low(s + 2, p, 1)
                    norm_full(s + 2, p)

            router_steps = [0]

            def small(ins):
                ins.then_inc(rt_done, 1)
                router_steps[0] += 1
                dve.wait_ge(rt_done, router_steps[0])

            def wide(pairs):
                return top[:, pairs].unsqueeze(2).broadcast_to([P, pairs.stop - pairs.start, E_ROUTED])

            def router_start(pairs):
                dve.wait_ge(logits_free, pairs.stop + 1)
                small(dve.tensor_reduce(top[:, pairs], logit[:, pairs, :], AX.X, ALU.max))
                dve.tensor_tensor(left[:, pairs, :], logit[:, pairs, :], wide(pairs), ALU.subtract).then_inc(left_done, 1)

            def router_pick(part, pairs):
                scores_, left_, hit_ = score[:, pairs, :], left[:, pairs, :], hit[:, pairs, :]
                pick_ = pick[:, pairs, :]
                rank = kst[:, K_RANK:K_RANK + E_ROUTED].unsqueeze(1).broadcast_to([P, pairs.stop - pairs.start, E_ROUTED])
                dve.wait_ge(rexp_done, part + 1)
                small(dve.tensor_reduce(top[:, pairs], scores_, AX.X, ALU.add))
                small(dve.reciprocal(top[:, pairs], top[:, pairs]))
                small(dve.tensor_tensor(scores_, scores_, wide(pairs), ALU.mult))
                src = scores_
                for t in range(2):
                    small(dve.tensor_reduce(top[:, pairs], src, AX.X, ALU.max))
                    small(dve.tensor_tensor(hit_, src, wide(pairs), ALU.is_equal))
                    small(dve.tensor_tensor(hit_, hit_, rank, ALU.mult))
                    small(dve.tensor_reduce(top[:, pairs], hit_, AX.X, ALU.max))
                    small(dve.tensor_tensor(pick_ if t == 0 else hit_, hit_, wide(pairs), ALU.is_equal))
                    if t == 0:
                        small(dve.scalar_tensor_tensor(out=left_, in0=pick_, scalar=-2.0, in1=scores_, op0=ALU.mult, op1=ALU.add))
                        src = left_
                small(dve.tensor_tensor(hit_, pick_, hit_, ALU.add))
                small(dve.scalar_tensor_tensor(out=comb[:, pairs, 0:E_ROUTED], in0=hit_, scalar=hgf[:, 0:1], in1=scores_, op0=ALU.mult, op1=ALU.mult))

            def hidden(k, j):
                q, r = j % 2, j % 4
                dve.wait_ge(th_done, k + 1)
                dve.scalar_tensor_tensor(out=hs[q], in0=th[q], scalar=1.0, in1=ps[q][:, :], op0=ALU.add, op1=ALU.mult).then_inc(hs_done, 1)
                dve.wait_ge(hs_done, k + 1)
                need(dve, glo_done, k - 3)
                dve.tensor_tensor(g[r], hs[q], pt[q][:, :], ALU.mult).then_inc(g_done, 1)

            def add_expert(k, j, e):
                for half in range(2):
                    dve.wait_ge(y2_filled, 2 * k + half + 1)
                    need(dve, y2_done, 2 * k + half - 1)
                    for t in range(2):
                        tile = TILES * (j % CHUNKS) + 2 * half + t
                        mm = dve.scalar_tensor_tensor(out=x1[:, tile, :], in0=y_banks[j % 2][half][:, D * t:D * t + D],
                                                      scalar=comb[:, tile, bass.ds(e, 1)], in1=x1[:, tile, :], op0=ALU.mult, op1=ALU.add)
                    mm.then_inc(y2_done, 1)

            def finish():
                recip(B - 1, 0)
                recip(B - 1, 1)
                rz_split(B - 1)
                hidden(0, 0)
                divide(B - 1, 1, 0)
                divide(B - 1, 1, 1)
                hidden(1, 1)
                residual(PAIRS - 1)
                need(dve, res_done, PAIRS)
                token_stats(PAIRS - 1)
                need(dve, bnt_done, PAIRS)
                token_aggregate()
                token_norm(PAIRS - 1)
                hidden(2, 2)
                logits_out(PAIRS - 1)
                router_start(slice(EARLY, PAIRS))
                add_expert(0, 0, 0)
                hidden(3, 3)
                router_pick(1, slice(EARLY, PAIRS))

                def unit(k, j, step):
                    hidden(k, j)
                    add_expert(k - LAG - 1, j + 1, 2 * step + (j + 1) // CHUNKS)

                expert_loop(dve, unit)
                for k in range(CHUNKS * EXPERTS - LAG - 1, CHUNKS * EXPERTS):
                    add_expert(k, k, EXPERTS - 1)

            body_loop(dve, step, finish)

        @block.gpsimd
        def _(pool):
            pool.memset(minus_half[:, :], -0.5).then_inc(zero_done, 1)
            pool.memset(eps[:, :], EPS).then_inc(zero_done, 1)

            def rstd_of(b, q):
                need(pool, stats_done, b + 1)
                need(pool, xn_done, b - 1)
                pool.tensor_tensor(ve[q][:, :], mv[q][:, 1:2], eps[:, :], ALU.add).then_inc(ve_done, 1)
                need(pool, ve_done, b + 1)
                pool.tensor_tensor(rstd[q][:, :], ve[q][:, :], minus_half[:, :], ALU.pow).then_inc(rstd_done, 1)

            def context_low(b, q):
                need(pool, ch_done, b + 1)
                pool.tensor_tensor(cl[q][:, :], raw_c[q][:, :], ch[q][:, :].bitcast(F32), ALU.subtract).then_inc(cl_done, 1)

            def x_low(b, q):
                need(pool, xn_done, b + 1)
                need(pool, st_done, 8 * (b - 1))
                pool.tensor_tensor(xlm[q][0:C, :], xn[:, :], xh[q][0:C, :].bitcast(F32), ALU.subtract).then_inc(xl_done, 1)

            pool.wait_ge(zero_done, 5)
            context_low(0, 0)
            rstd_of(0, 0)
            rstd_of(1, 1)
            x_low(0, 0)
            context_low(1, 1)
            pool.wait_ge(tg_done, 1)

            def add_keys(s, h):
                need(pool, exp_done, 8 * s + h + 1)
                if h % 4 == 0:
                    need(pool, z_done, 2 * s + h // 4)
                pool.tensor_tensor(ez[h % 4][:, :], ex[h][:, 0, :], ex[h][:, 1, :], ALU.add).then_inc(ez_done, 1)

            def add_heads(f, fp, folded):
                need(pool, mul_done, 2 * f + 2)
                o = os_[fp]
                pool.tensor_tensor(o[:, 0:2, :].rearrange("p k i -> p (k i)"), o[:, 0:2, :].rearrange("p k i -> p (k i)"),
                                   o[:, 2:4, :].rearrange("p k i -> p (k i)"), ALU.add).then_inc(add_done, 1)
                need(pool, add_done, f + 1)
                need(pool, y_done, folded)
                pool.tensor_tensor(acc[fp][:, :], o[:, 0, :], o[:, 1, :], ALU.add).then_inc(sum_done, 1)

            def weights_low(e, q):
                need(pool, wh_done, e + 1)
                pool.tensor_tensor(w_lo[q][:, :], w_raw[q][:, :], w_hi[q][:, :].bitcast(F32), ALU.subtract).then_inc(wl_done, 1)

            def residual_x(it):
                need(pool, xr_in, 16 * (it + 1))
                pool.tensor_tensor(xr[:, :], xr[:, :], tgb[:, :].broadcast_to([P, N]), ALU.add).then_inc(xr_done, 1)

            def token_rstd(pair):
                need(pool, statt_done, pair + 1)
                pool.tensor_tensor(vet[:, :], mvt[:, 1:2], eps[:, :], ALU.add).then_inc(vet_done, 1)
                need(pool, vet_done, pair + 1)
                need(pool, xn2_done, pair)
                pool.tensor_tensor(rstdt[:, :], vet[:, :], minus_half[:, :], ALU.pow).then_inc(rstdt_done, 1)

            def token_low(pair):
                cols = bass.ds(P * pair, P)
                need(pool, xth_done, pair + 1)
                pool.tensor_tensor(xtl[:, :, cols], xt[:, :, :], xth[:, :, cols].bitcast(F32), ALU.subtract).then_inc(xtl_done, 1)

            def step(it, p):
                s, q = 2 * it + p, 1 - p
                n, f = s + 1, s - 1
                fin = not isinstance(s, int) or s > 0
                late = not isinstance(it, int) or it > 0
                tok = p == 1 and late
                if fin:
                    for h in range(6, 8):
                        add_keys(f, h)
                if known(n, B):
                    x_low(n, q)
                add_keys(s, 0)
                if p == 0 and late:
                    residual_x(it - 1)
                add_keys(s, 1)
                add_keys(s, 2)
                if known(s + 2, B):
                    rstd_of(s + 2, p)
                if tok:
                    token_rstd(it - 1)
                add_keys(s, 3)
                if known(s + 2, B):
                    context_low(s + 2, p)
                if fin:
                    add_heads(f, q, it if p == 1 else it - 1)
                for h in range(4, 6):
                    add_keys(s, h)
                if tok:
                    token_low(it - 1)
                if not known(s + 2, B):
                    weights_low(p, p)

            def hidden_low(k, j):
                pool.wait_ge(ghi_done, k + 1)
                need(pool, y2_filled, 2 * (k - 3))
                pool.tensor_tensor(gl[j % 4], g[j % 4], gh[j % 4].bitcast(F32), ALU.subtract).then_inc(glo_done, 1)

            def finish():
                for h in range(6, 8):
                    add_keys(B - 1, h)
                residual_x(PAIRS - 1)
                hidden_low(0, 0)
                add_heads(B - 1, 1, PAIRS - 1)
                token_rstd(PAIRS - 1)
                hidden_low(1, 1)
                token_low(PAIRS - 1)
                hidden_low(2, 2)
                hidden_low(3, 3)

                def unit(k, j, step):
                    e = 1 + 2 * step + j // CHUNKS
                    if j % CHUNKS == 2 and known(e + 1, EXPERTS):
                        weights_low(e + 1, j // CHUNKS)
                    hidden_low(k, j)

                expert_loop(pool, unit)

            body_loop(pool, step, finish)


def kernel(**inputs):
    from concourse import bacc
    from concourse.bass_utils import run_bass_kernel_spmd

    def get(name):
        return np.ascontiguousarray(inputs[name])

    w1 = np.concatenate([get("L0_ffn_w1"), get("L0_ffn_ws1")[None]])
    w3 = np.concatenate([get("L0_ffn_w3"), get("L0_ffn_ws3")[None]])
    w2 = np.concatenate([get("L0_ffn_w2"), get("L0_ffn_ws2")[None]])
    w13T = np.stack([w1, w3], axis=1).reshape(EXPERTS, 2, INTER, DB, P).transpose(0, 4, 1, 3, 2).reshape(EXPERTS, P, -1)
    w2T = w2.transpose(0, 2, 1)
    arrays = {
        "x": get("x"), "ctx_in": get("ctx_2048"), "g_xattn": get("g_xattn"), "g_ffn": get("g_ffn"),
        "wq": get("L0_xattn_Wq"), "wk": get("L0_xattn_Wkv")[:HEADS * DH], "wv": get("L0_xattn_Wkv")[HEADS * DH:],
        "woT": get("L0_xattn_Wout").T, "bout": get("L0_xattn_bout"), "gateT": get("L0_ffn_gate_w").T,
        "w_all": np.concatenate([w13T, w2T], axis=2), "consts": constants(),
    }
    arrays = {f"in_{k}": np.ascontiguousarray(a) for k, a in arrays.items()}
    nc = bacc.Bacc("TRN2", target_bir_lowering=False, num_devices=1)
    args = [nc.dram_tensor(k, a.shape, mybir.dt.from_np(a.dtype), kind="ExternalInput").ap() for k, a in arrays.items()]
    out = nc.dram_tensor("out", (B, C, N), F32, kind="ExternalOutput").ap()
    build(nc, *args, out)
    r = run_bass_kernel_spmd(nc, [arrays], core_ids=[0])
    return r.results[0]["out"]
```

```python
from contextlib import ExitStack

import numpy as np

import concourse.bass as bass
from concourse import mybir

F32 = mybir.dt.float32
F32R = mybir.dt.float32r
ALU = mybir.AluOpType
ACT = mybir.ActivationFunctionType
AX = mybir.AxisListType

P = 128
B, C, N = 32, 64, 256
HEADS, DH = 8, 64
E_ROUTED, INTER = 8, 128
EXPERTS = E_ROUTED + 1
D = N
PAIRS = B // 2
JB = N // P
DB = D // P
EPS = 1e-5
CHUNK = 512
TILES = CHUNK // P
CHUNKS = B * C // CHUNK
LAG = 2
EARLY = PAIRS - 2
W_COLS = 2 * DB * INTER + D

RING = ["G0", "S0", "S1", "G1", "S2", "S3", "S4", "S5", "S6", "S7"]
BANK = [0, 1, 2, 0, 1, 2, 0, 1, 2, 1]
RN = len(RING)
BANKS = 3

K_ID, K_HEAD, K_FOLD, K_DEN, K_RANK, K_LOW, K_PAIR = 0, 128, 136, 200, 264, 272, 273
K_KEPT = K_PAIR
K_COLS = K_PAIR + HEADS // 2 * P


def constants():
    k = np.zeros((P, K_COLS), np.float32)
    k[:, K_ID:K_ID + P] = np.eye(P)
    for h in range(HEADS):
        k[C * (1 - h % 2) + h, K_HEAD + h] = 1
        row, at = 32 * (h % 4) + h // 4, K_PAIR + P * (h // 2) + C * (h % 2)
        k[row, at:at + C] = k[row + 4, at:at + C] = 1
    k[:, K_FOLD:K_FOLD + C] = np.vstack([np.eye(C), np.eye(C)])
    for use in range(2):
        at = K_DEN + 32 * use
        k[:, at + use] = k[:, at + use + 4] = 1
    k[:, [K_DEN + t for t in range(32) if t not in (0, 1, 4, 5)]] = 1
    for t in range(4):
        k[32 * t + 4:32 * t + 8, K_LOW] = -1
    k[:, K_RANK:K_RANK + E_ROUTED] = E_ROUTED - np.arange(E_ROUTED)
    return k


def need(eng, sem, value):
    if not isinstance(value, int) or value > 0:
        eng.wait_ge(sem, value)


def build(nc, x, ctx_in, g_xattn, g_ffn, wq, wk, wv, woT, bout, gateT, w_all, consts, out):
    with ExitStack() as stack:
        def sb(name, shape, dt=F32):
            return stack.enter_context(nc.sbuf_tensor(name, shape, dt))

        def bank(name):
            return stack.enter_context(nc.psum_tensor(name, [P, 512], F32))

        def sem(name):
            return stack.enter_context(nc.semaphore(name))

        kst = sb("kst", [P, K_KEPT])
        ident_r = sb("ident_r", [P, P], F32R)
        pair_r = sb("pair_r", [P, HEADS // 2, P], F32R)
        mhl = sb("mhl", [P, HEADS, C], F32R)
        nhl = sb("nhl", [P, HEADS, C], F32R)
        gates = sb("gates", [P, 2])
        tg = sb("tg", [P, 2])
        bo = sb("bo", [P, 1])
        tgb = sb("tgb", [P, 1])
        hgf = sb("hgf", [P, 1])
        minus_half = sb("minus_half", [P, 1])
        eps = sb("eps", [P, 1])
        gate_t = sb("gate_t", [P, DB, E_ROUTED])
        w_raw = [sb(f"w_raw{q}", [P, W_COLS]) for q in range(2)]
        w_hi = [sb(f"w_hi{q}", [P, W_COLS], F32R) for q in range(2)]
        w_lo = [sb(f"w_lo{q}", [P, W_COLS], F32R) for q in range(2)]
        x1 = sb("x1", [P, PAIRS, D])
        bn6t = sb("bn6t", [P, 6])
        mvt = sb("mvt", [P, 2])
        vet = sb("vet", [P, 1])
        rstdt = sb("rstdt", [P, 1])
        xn2 = sb("xn2", [P, D])
        xt = sb("xt", [P, DB, P])
        xth = sb("xth", [P, DB, B * C], F32R)
        xtl = sb("xtl", [P, DB, B * C], F32R)
        logit = sb("logit", [P, PAIRS, E_ROUTED])
        top = sb("top", [P, PAIRS])
        score = sb("score", [P, PAIRS, E_ROUTED])
        left = sb("left", [P, PAIRS, E_ROUTED])
        hit = sb("hit", [P, PAIRS, E_ROUTED])
        pick = sb("pick", [P, PAIRS, E_ROUTED])
        comb = sb("comb", [P, PAIRS, EXPERTS])

        raw_x = [sb(f"raw_x{q}", [P, N]) for q in range(2)]
        raw_c = [sb(f"raw_c{q}", [P, N]) for q in range(2)]
        bn6 = [sb(f"bn6_{q}", [P, 6]) for q in range(2)]
        mv = [sb(f"mv{q}", [P, 2]) for q in range(2)]
        ve = [sb(f"ve{q}", [P, 1]) for q in range(2)]
        rstd = [sb(f"rstd{q}", [P, 1]) for q in range(2)]
        xn = sb("xn", [P, N])
        xh = [sb(f"xh{q}", [P, N], F32R) for q in range(2)]
        xlm = [sb(f"xlm{q}", [P, N], F32R) for q in range(2)]
        mxl = [sb(f"mxl{q}", [P, N], F32R) for q in range(2)]
        ch = [sb(f"ch{q}", [P, N], F32R) for q in range(2)]
        cl = [sb(f"cl{q}", [P, N], F32R) for q in range(2)]
        ghl = [sb(f"ghl{q}", [P, HEADS, N], F32R) for q in range(2)]
        ghs = [sb(f"ghs{q}", [P, HEADS, N], F32R) for q in range(2)]
        u = [sb(f"u{q}", [P, JB, HEADS, C]) for q in range(2)]
        nmax = sb("nmax", [P, JB, P], F32R)
        ex = [sb(f"ex{h}", [P, JB, N]) for h in range(HEADS)]
        wk2, wv2 = (ex[h].rearrange("p b (k c) -> p (b k) c", c=2 * C).rearrange("p k (r c) -> p k r c", r=2) for h in (1, 2))
        wq_ = ex[0][:, 0, :].rearrange("p (k c) -> p k c", c=C)
        wo = ex[3][:, 0, :].rearrange("p (k c) -> p k c", c=C)
        k_pair = ex[4].rearrange("p b i -> p (b i)")
        ez = [sb(f"ez{t}", [P, N]) for t in range(4)]
        os_ = [sb(f"os{q}", [P, HEADS // 2, N]) for q in range(2)]
        rz = sb("rz", [P, N])
        rzh = sb("rzh", [P, N], F32R)
        rzc = sb("rzc", [P, N], F32R)
        acc = [sb(f"acc{q}", [P, N]) for q in range(2)]
        xr = sb("xr", [P, N])
        ps = [bank(f"ps{t}") for t in range(BANKS)]
        pt = [bank("pt0"), bank("pt1")]
        po, pz, pm = bank("po"), bank("pz"), bank("pm")
        th, hs, g = ([ex[h].rearrange("p b i -> p (b i)") for h in hs_] for hs_ in ((0, 1), (2, 3), (4, 5, 6, 7)))
        gh, gl = ([t[:, JB * r:JB * r + 2, :].rearrange("p h j -> p (h j)") for r in range(4)] for t in (ghl[0], ghs[0]))
        y_banks = [(ps[2], pz), (po, pm)]

        wqk_in = sem("wqk_in")
        wvo_in = sem("wvo_in")
        const_in = sem("const_in")
        pairs_in = sem("pairs_in")
        sel_done = sem("sel_done")
        small_in = sem("small_in")
        w_in = [sem(f"w_in{q}") for q in range(2)]
        consts_done = sem("consts_done")
        zero_done = sem("zero_done")
        tanh_done = sem("tanh_done")
        tg_done = sem("tg_done")
        mprod_done = sem("mprod_done")
        mhi_done = sem("mhi_done")
        mhl_done = sem("mhl_done")
        nprod_done = sem("nprod_done")
        nhi_done = sem("nhi_done")
        nhl_done = sem("nhl_done")
        x_in = [sem(f"x_in{q}") for q in range(2)]
        c_in = [sem(f"c_in{q}") for q in range(2)]
        xr_in = sem("xr_in")
        bn_done = sem("bn_done")
        stats_done = sem("stats_done")
        ve_done = sem("ve_done")
        rstd_done = sem("rstd_done")
        xh_done = sem("xh_done")
        xn_done = sem("xn_done")
        xl_done = sem("xl_done")
        ch_done = sem("ch_done")
        cl_done = sem("cl_done")
        ring_filled = sem("ring_filled")
        u_filled = sem("u_filled")
        gh_done = sem("gh_done")
        gs_done = sem("gs_done")
        gl_done = sem("gl_done")
        u_done = sem("u_done")
        max_done = sem("max_done")
        mt_filled = sem("mt_filled")
        mt_done = sem("mt_done")
        st_done = sem("st_done")
        exp_done = sem("exp_done")
        av_done = sem("av_done")
        z_done = sem("z_done")
        os_done = sem("os_done")
        recip_done = sem("recip_done")
        rzh_done = sem("rzh_done")
        rzc_done = sem("rzc_done")
        ez_done = sem("ez_done")
        rb_done = sem("rb_done")
        mul_done = sem("mul_done")
        add_done = sem("add_done")
        sum_done = sem("sum_done")
        y_done = sem("y_done")
        xr_done = sem("xr_done")
        res_done = sem("res_done")
        bnt_done = sem("bnt_done")
        statt_done = sem("statt_done")
        vet_done = sem("vet_done")
        rstdt_done = sem("rstdt_done")
        xn2_done = sem("xn2_done")
        tr_done = sem("tr_done")
        xt_done = sem("xt_done")
        xth_done = sem("xth_done")
        xtl_done = sem("xtl_done")
        lg_filled = sem("lg_filled")
        logits_free = sem("logits_free")
        wh_done = sem("wh_done")
        wl_done = sem("wl_done")
        rt_done = sem("rt_done")
        left_done = sem("left_done")
        rexp_done = sem("rexp_done")
        hu_filled = sem("hu_filled")
        th_done = sem("th_done")
        hs_done = sem("hs_done")
        g_done = sem("g_done")
        ghi_done = sem("ghi_done")
        glo_done = sem("glo_done")
        y2_filled = sem("y2_filled")
        y2_done = sem("y2_done")
        out_done = sem("out_done")

        def body_loop(eng, step, finish):
            step(0, 0)
            step(0, 1)
            with eng.Fori(1, PAIRS - 1) as it:
                step(it, 0)
                step(it, 1)
            step(PAIRS - 1, 0)
            step(PAIRS - 1, 1)
            finish()

        def known(v, limit):
            return not isinstance(v, int) or v < limit

        def w1_of(w, m, db):
            return w[:, (m * DB + db) * INTER:(m * DB + db + 1) * INTER]

        def w2_of(w):
            return w[:, 2 * DB * INTER:]

        def expert_loop(eng, unit):
            steps = (EXPERTS - 1) // 2
            with eng.Fori(0, steps - 1) as it:
                for j in range(2 * CHUNKS):
                    unit(CHUNKS + 2 * CHUNKS * it + j, j, it)
            for j in range(2 * CHUNKS):
                unit(CHUNKS + 2 * CHUNKS * (steps - 1) + j, j, steps - 1)

        block = stack.enter_context(nc.Block())

        @block.sync
        def _(sp):
            def load(b, q, b_after):
                need(sp, xn_done, b_after)
                sp.dma_start(raw_x[q][:, :], twice(x, b)).then_inc(x_in[q], 16)
                need(sp, cl_done, b_after)
                sp.dma_start(raw_c[q][:, :], twice(ctx_in, b)).then_inc(c_in[q], 16)

            def twice(t, b):
                return t[bass.ds(b, 1), :, :].broadcast_to([2, C, N])

            def projection(t, w, done):
                sp.dma_start(t, w.rearrange("(k p) c -> p k c", p=P)).then_inc(done, 16)

            for r in range(2):
                projection(wk2[:, :, r, :], wk, wqk_in)
            projection(wq_[:, :, :], wq, wqk_in)
            load(0, 0, 0)
            for r in range(2):
                projection(wv2[:, :, r, :], wv, wvo_in)
            projection(wo[:, :, :], woT, wvo_in)
            sp.dma_start(kst[:, :], consts[:, 0:K_KEPT]).then_inc(const_in, 16)
            load(1, 1, 0)
            sp.dma_start(k_pair, consts[:, K_PAIR:K_COLS]).then_inc(pairs_in, 16)
            for t, g in enumerate((g_xattn, g_ffn)):
                sp.dma_start(gates[:, t:t + 1], g.rearrange("(a o) -> a o", a=1).broadcast_to([P, 1])).then_inc(small_in, 16)
            for r in (0, C):
                sp.dma_start(bo[r:r + C, :], bout.rearrange("(c o) -> c o", o=1)).then_inc(small_in, 16)
            sp.dma_start(gate_t[:, :, :], gateT.rearrange("(k p) e -> p k e", p=P)).then_inc(small_in, 16)

            def weights(e, q):
                need(sp, wl_done, e - 1)
                sp.dma_start(w_raw[q][:, :], w_all[bass.ds(e, 1), :, :].rearrange("o p w -> (o p) w")).then_inc(w_in[q], 16)

            weights(0, 0)
            weights(1, 1)

            def step(it, p):
                s = 2 * it + p
                if known(s + 2, B):
                    load(s + 2, p, s + 1)
                if p == 1:
                    need(sp, res_done, it)
                    sp.dma_start(xr[:, :], x[bass.ds(2 * it, 2), :, :].rearrange("b c n -> (b c) n")).then_inc(xr_in, 16)

            def finish():
                with sp.Fori(1, EXPERTS // 2) as i:
                    weights(2 * i, 0)
                    weights(2 * i + 1, 1)
                weights(EXPERTS - 1, 0)
                o_rows = out.rearrange("(t b) c n -> (b c) t n", b=2)
                last = CHUNKS * (EXPERTS - 1)
                for c in range(CHUNKS):
                    for half in range(2):
                        sp.wait_ge(y2_done, 2 * (last + c) + half + 1)
                        tiles = slice(TILES * c + 2 * half, TILES * c + 2 * half + 2)
                        sp.dma_start(o_rows[:, tiles, :], x1[:, tiles, :]).then_inc(out_done, 16)
                sp.wait_ge(out_done, 16 * 2 * CHUNKS)

            body_loop(sp, step, finish)

        @block.tensor
        def _(pe):
            pe.wait_ge(wqk_in, 16 * 3)
            for h in range(HEADS):
                r, k = DH * (h % 2), h // 2
                mm = pe.matmul(ps[h % 2][:, C * k:C * k + C], wk2[r:r + DH, k, :, :].rearrange("d r c -> d (r c)"),
                               wq_[r:r + DH, k, :], start=True, stop=True)
            mm.then_inc(mprod_done, 1)

            def value_products(odd):
                rows = slice(DH * odd, DH * odd + DH)
                for k in range(HEADS // 2):
                    mm = pe.matmul(pt[odd][:, C * k:C * k + C], wv2[rows, k, :, :].rearrange("d r c -> d (r c)"),
                                   wo[rows, k, :], start=True, stop=True)
                mm.then_inc(nprod_done, 1)

            def ring(use, b, q):
                k = RING.index(use)
                bank_ = ps[BANK[k]]
                last = max([t for t in range(k) if BANK[t] == BANK[k]], default=-1)
                back = b
                if last < 0:
                    last, back = max(t for t in range(RN) if BANK[t] == BANK[k]), b - 1
                i = int(RING[last][1])
                if RING[last][0] == "G":
                    need(pe, gl_done, 4 * back + 2 * i + 2)
                else:
                    need(pe, max_done, 8 * back + i + 1)
                i = int(use[1])
                if use[0] == "G":
                    need(pe, cl_done, b + 1)
                    for t in range(2):
                        heads = mhl[:, 4 * i + 2 * t:4 * i + 2 * t + 2, :].rearrange("p h c -> p (h c)")
                        pe.matmul(bank_[:, N * t:N * t + N], heads, ch[q][:, :], start=True, stop=False)
                        mm = pe.matmul(bank_[:, N * t:N * t + N], heads, cl[q][:, :], start=False, stop=True)
                else:
                    need(pe, gl_done, 4 * b + 2 * (i // 4) + i % 2 + 1)
                    need(pe, xh_done, b + 1)
                    for ib in range(JB):
                        mm = pe.matmul(bank_[:, N * ib:N * ib + N], xh[q][:, P * ib:P * ib + P], ghl[q][:, i, :], start=True, stop=True)
                mm.then_inc(ring_filled, 1)

            def values(b, q, i, free_sem, free_at):
                need(pe, cl_done, b + 1)
                need(pe, free_sem, free_at)
                js = slice(P * i, P * i + P)
                pe.matmul(po[:, :], ch[q][:, js], nhl[:, :, :].rearrange("p h c -> p (h c)"), start=True, stop=False)
                pe.matmul(po[:, :], cl[q][:, js], nhl[:, :, :].rearrange("p h c -> p (h c)"), start=False, stop=True).then_inc(u_filled, 1)

            def max_rows(b, free_sem, free_at):
                need(pe, max_done, 8 * b + 8)
                need(pe, free_sem, free_at)
                for ib in range(JB):
                    mm = pe.matmul(pm[:, P * ib:P * ib + P], nmax[:, ib, :], ident_r[:, :], start=True, stop=True)
                mm.then_inc(mt_filled, 1)

            def scores(s, p, h):
                if h < 2:
                    need(pe, xl_done, 2 * s + h + 1)
                    need(pe, mt_done, 2 * s + h + 1)
                    need(pe, gs_done, 4 * s + 4)
                low = (xlm, mxl)[h % 2][p]
                need(pe, exp_done, 8 * s + h - 1)
                for jb in range(JB):
                    js = slice(P * jb, P * jb + P)
                    pe.matmul(pt[h % 2][:, N * jb:N * jb + N], ghl[p][:, h, js], xh[p][:, :], start=True, stop=False)
                    mm = pe.matmul(pt[h % 2][:, N * jb:N * jb + N], ghs[p][:, h, js], low[:, :], start=False, stop=True)
                mm.then_inc(st_done, 1)

            def weighted(s, p, k, free_sem, free_at):
                need(pe, exp_done, 8 * s + 2 * k + 2)
                need(pe, u_done, 2 * s + 2)
                need(pe, free_sem, free_at)
                for jb in range(JB):
                    for r in range(2):
                        h = 2 * k + r
                        mm = pe.matmul(po[C * r:C * r + C, 0:N], u[p][:, jb, h, :], ex[h][:, jb, :],
                                       start=(jb == 0), stop=(jb == JB - 1))
                mm.then_inc(av_done, 1)

            def denominators(s, k):
                need(pe, ez_done, 8 * s + 4 * k + 4)
                if k == 0:
                    need(pe, recip_done, 2 * s)
                at = K_DEN + 32 * k
                for t in range(4):
                    mm = pe.matmul(pz[32 * t:32 * t + 32, 0:N], kst[:, at:at + 32], ez[t][:, :], start=(k == 0), stop=(k == 1))
                mm.then_inc(z_done, 1)

            def spread(f, k, free_sem, free_at, bank_=pm):
                need(pe, rzc_done, f + 1)
                need(pe, free_sem, free_at)
                for r in range(2):
                    mm = pe.matmul(bank_[:, N * r:N * r + N], pair_r[:, 2 * k + r, :], rzc[:, :], start=True, stop=True)
                mm.then_inc(rb_done, 1)

            def fold(pair, free_sem, free_at):
                need(pe, sum_done, 2 * pair + 2)
                need(pe, free_sem, free_at)
                for r in range(2):
                    mm = pe.matmul(pm[C * r:C * r + C, 0:N], kst[:, K_FOLD:K_FOLD + C], acc[r][:, :], start=True, stop=True)
                mm.then_inc(y_done, 1)

            def turn(pair, free_sem, free_at):
                need(pe, xn2_done, pair + 1)
                need(pe, free_sem, free_at)
                for db in range(DB):
                    mm = pe.transpose(po[:, P * db:P * db + P], xn2[:, P * db:P * db + P], kst[:, K_ID:K_ID + P])
                mm.then_inc(tr_done, 1)

            def route(pair):
                need(pe, xt_done, pair + 1)
                for db in range(DB):
                    mm = pe.matmul(po[:, 0:E_ROUTED], xt[:, db, :], gate_t[:, db, :], start=(db == 0), stop=(db == DB - 1))
                mm.then_inc(lg_filled, 1)

            pe.wait_ge(wvo_in, 16 * 3)
            value_products(0)
            pe.wait_ge(mhl_done, 2)
            pe.wait_ge(zero_done, 7)
            ring("G0", 0, 0)
            value_products(1)
            for use in RING[1:8]:
                ring(use, 0, 0)
            pe.wait_ge(nhl_done, 2)
            values(0, 0, 0, mhl_done, 0)
            ring("S6", 0, 0)
            values(0, 0, 1, u_done, 1)
            ring("S7", 0, 0)
            ring("G0", 1, 1)
            pe.wait_ge(consts_done, 2)
            pe.wait_ge(sel_done, 2)
            max_rows(0, mhl_done, 0)

            def step(it, p):
                s, q = 2 * it + p, 1 - p
                n, f = s + 1, s - 1
                nxt = known(n, B)
                fin = not isinstance(s, int) or s > 0
                tok = p == 1 and (not isinstance(it, int) or it > 0)

                def r(*uses):
                    if nxt:
                        for use in uses:
                            ring(use, n, q)

                if fin:
                    if p == 0:
                        pe.wait_ge(logits_free, it)
                    weighted(f, q, 2, os_done, 4 * f + 2)
                r("S0")
                scores(s, p, 0)
                r("S1")
                scores(s, p, 1)
                if fin:
                    weighted(f, q, 3, os_done, 4 * f + 3)
                    denominators(f, 1)
                if nxt:
                    values(n, q, 0, *((os_done, 4 * s) if fin else (u_done, 2)))
                r("G1", "S2")
                scores(s, p, 2)
                scores(s, p, 3)
                if tok:
                    fold(it - 1, mt_done, 2 * s + 2)
                weighted(s, p, 0, *((u_done, 2 * n + 1) if nxt else (os_done, 4 * s)))
                r("S3")
                scores(s, p, 4)
                scores(s, p, 5)
                r("S4")
                if fin:
                    spread(f, 0, *((res_done, it) if tok else (mt_done, 2 * s + 2)))
                if nxt:
                    values(n, q, 1, os_done, 4 * s + 1)
                r("S5")
                denominators(s, 0)
                r("S6")
                if fin:
                    spread(f, 1, mul_done, 2 * f + 1)
                weighted(s, p, 1, *((u_done, 2 * n + 2) if nxt else (os_done, 4 * s + 1)))
                r("S7")
                scores(s, p, 6)
                if tok:
                    turn(it - 1, os_done, 4 * s + 2)
                if known(s + 2, B):
                    ring("G0", s + 2, p)
                scores(s, p, 7)
                if tok:
                    route(it - 1)
                if nxt:
                    max_rows(n, mul_done, 2 * f + 2)

            def first(k, j, e, q):
                c = j % CHUNKS
                if isinstance(e, int) and e == 0:
                    pe.wait_ge(xtl_done, TILES * (c + 1))
                if c == 0:
                    pe.wait_ge(wl_done, e + 1)
                need(pe, g_done, k - 1)
                cols = slice(CHUNK * c, CHUNK * (c + 1))
                for m, bank_ in enumerate((ps[j % 2], pt[j % 2])):
                    for db in range(DB):
                        pe.matmul(bank_[:, :], w1_of(w_hi[q], m, db), xth[:, db, cols], start=(db == 0), stop=False)
                        pe.matmul(bank_[:, :], w1_of(w_hi[q], m, db), xtl[:, db, cols], start=False, stop=False)
                        mm = pe.matmul(bank_[:, :], w1_of(w_lo[q], m, db), xth[:, db, cols], start=False, stop=(db == DB - 1))
                mm.then_inc(hu_filled, 1)

            def second(k, j, q):
                r = j % 4
                pe.wait_ge(glo_done, k + 1)
                for half in range(2):
                    bank_ = y_banks[j % 2][half]
                    need(pe, y2_done, 2 * (k - LAG) + half + 1)
                    for t in range(2):
                        o = bank_[:, D * t:D * t + D]
                        rows = slice(P * (2 * half + t), P * (2 * half + t) + P)
                        pe.matmul(o, gh[r][:, rows], w2_of(w_hi[q]), start=True, stop=False)
                        pe.matmul(o, gh[r][:, rows], w2_of(w_lo[q]), start=False, stop=False)
                        mm = pe.matmul(o, gl[r][:, rows], w2_of(w_hi[q]), start=False, stop=True)
                    mm.then_inc(y2_filled, 1)

            def finish():
                pe.wait_ge(logits_free, PAIRS)
                weighted(B - 1, 1, 2, os_done, 4 * B - 2)
                weighted(B - 1, 1, 3, os_done, 4 * B - 1)
                denominators(B - 1, 1)
                first(0, 0, 0, 0)
                spread(B - 1, 0, mul_done, 2 * B - 2)
                spread(B - 1, 1, recip_done, 2 * B, pz)
                first(1, 1, 0, 0)
                fold(PAIRS - 1, mul_done, 2 * B)
                first(2, 2, 0, 0)
                second(0, 0, 0)
                turn(PAIRS - 1, os_done, 4 * B)
                route(PAIRS - 1)
                pe.wait_ge(logits_free, PAIRS + 1)
                pe.wait_ge(res_done, PAIRS)
                second(1, 1, 0)
                first(3, 3, 0, 0)

                def unit(k, j, step):
                    first(k, j, 1 + 2 * step + j // CHUNKS, (1 + j // CHUNKS) % 2)
                    second(k - LAG, j + LAG, (j + LAG) // CHUNKS % 2)

                expert_loop(pe, unit)
                for k in range(CHUNKS * EXPERTS - LAG, CHUNKS * EXPERTS):
                    second(k, k, 0)

            body_loop(pe, step, finish)

        @block.scalar
        def _(act):
            def g_high(b, q, i, odd):
                need(act, ring_filled, RN * b + RING.index(f"G{i}") + 1)
                need(act, st_done, 8 * (b - 1))
                rows = slice(C * odd, C * odd + C)
                src = ps[BANK[RING.index(f"G{i}")]][rows, :].rearrange("p (h j) -> p h j", j=N)
                act.activation(ghl[q][rows, 4 * i + odd:4 * i + 4:2, :], src, ACT.Copy).then_inc(gh_done, 1)

            def g_again(b, q, i, odd):
                need(act, gh_done, 4 * b + 2 * i + odd + 1)
                rows, heads = slice(C * odd, C * odd + C), slice(4 * i + odd, 4 * i + 4, 2)
                act.activation(ghs[q][rows, heads, :], ghl[q][rows, heads, :].bitcast(F32), ACT.Copy).then_inc(gs_done, 1)

            def u_out(b, q, i):
                need(act, u_filled, 2 * b + i + 1)
                act.activation(u[q][:, i, :, :].rearrange("p h c -> p (h c)"), po[:, :], ACT.Copy).then_inc(u_done, 1)

            def max_in(b, q):
                need(act, mt_filled, b + 1)
                act.activation(xlm[q][C:C + HEADS, :], pm[C:C + HEADS, 0:N], ACT.Copy).then_inc(mt_done, 1)
                act.activation(mxl[q][0:HEADS, :], pm[0:HEADS, 0:N], ACT.Copy).then_inc(mt_done, 1)

            def context_high(b, q, i):
                need(act, c_in[q], 16 * i)
                need(act, u_filled, 2 * (b - 1))
                act.activation(ch[q][:, :], raw_c[q][:, :], ACT.Copy).then_inc(ch_done, 1)

            def weights_high(e, q, i):
                need(act, w_in[q], 16 * i)
                need(act, y2_filled, 2 * CHUNKS * (e - 1))
                act.activation(w_hi[q][:, :], w_raw[q][:, :], ACT.Copy).then_inc(wh_done, 1)

            def expo(s, h):
                need(act, st_done, 8 * s + h + 1)
                need(act, av_done, 4 * (s - 1) + h // 2 + 1)
                need(act, ez_done, 8 * (s - 1) + h + 1)
                act.activation(ex[h][:, :, :].rearrange("p b i -> p (b i)"), pt[h % 2][:, :], ACT.Exp).then_inc(exp_done, 1)

            def sums_out(s, p, k):
                need(act, av_done, 4 * s + k + 1)
                if k == 0:
                    need(act, sum_done, s - 1)
                act.activation(os_[p][:, k, :], po[:, 0:N], ACT.Copy).then_inc(os_done, 1)

            def rz_high(f):
                need(act, recip_done, 2 * f + 2)
                need(act, rzc_done, f)
                act.activation(rzh[:, :], rz[:, :], ACT.Copy).then_inc(rzh_done, 1)

            def turned(pair):
                need(act, tr_done, pair + 1)
                need(act, lg_filled, pair)
                need(act, xtl_done, pair)
                act.activation(xt[:, :, :].rearrange("p b t -> p (b t)"), po[:, 0:D], ACT.Copy).then_inc(xt_done, 1)

            def turned_high(pair):
                need(act, xt_done, pair + 1)
                act.activation(xth[:, :, bass.ds(P * pair, P)], xt[:, :, :], ACT.Copy).then_inc(xth_done, 1)

            def selectors(q):
                for odd in range(2):
                    rows = slice(C * (1 - odd), C * (2 - odd))
                    act.activation(ghs[q][rows, odd:HEADS:2, :],
                                   kst[rows, K_HEAD + odd:K_HEAD + HEADS:2].unsqueeze(2).broadcast_to([C, HEADS // 2, N]),
                                   ACT.Copy).then_inc(sel_done, 1)

            context_high(0, 0, 1)
            act.wait_ge(mprod_done, 1)
            for r in range(2):
                act.activation(mhl[:, r:HEADS:2, :], ps[r][:, 0:4 * C].rearrange("p (k c) -> p k c", c=C), ACT.Copy).then_inc(mhi_done, 1)
            for odd in range(2):
                g_high(0, 0, 0, odd)
            for r in range(2):
                act.wait_ge(nprod_done, r + 1)
                act.activation(nhl[:, r:HEADS:2, :], pt[r][:, 0:4 * C].rearrange("p (k c) -> p k c", c=C), ACT.Copy).then_inc(nhi_done, 1)
            context_high(1, 1, 1)
            for odd in range(2):
                g_high(0, 0, 1, odd)
            act.wait_ge(const_in, 16)
            selectors(0)
            act.wait_ge(small_in, 16 * 5)
            act.activation(tg[:, :], gates[:, :], ACT.Tanh).then_inc(tanh_done, 1)
            for i in range(2):
                for odd in range(2):
                    g_again(0, 0, i, odd)
            u_out(0, 0, 0)
            u_out(0, 0, 1)
            for odd in range(2):
                g_high(1, 1, 0, odd)
            max_in(0, 0)
            selectors(1)

            def step(it, p):
                s, q = 2 * it + p, 1 - p
                n, f = s + 1, s - 1
                nxt = known(n, B)
                fin = not isinstance(s, int) or s > 0
                tok = p == 1 and (not isinstance(it, int) or it > 0)

                if fin:
                    sums_out(f, q, 2)
                if nxt:
                    g_again(n, q, 0, 1)
                expo(s, 0)
                if nxt:
                    g_again(n, q, 0, 0)
                if fin:
                    sums_out(f, q, 3)
                expo(s, 1)
                if not nxt:
                    router_exp(0, slice(0, EARLY))
                if nxt:
                    u_out(n, q, 0)
                    g_high(n, q, 1, 0)
                    g_high(n, q, 1, 1)
                expo(s, 2)
                expo(s, 3)
                if fin:
                    rz_high(f)
                sums_out(s, p, 0)
                if not known(s + 2, B):
                    weights_high(p, p, 1)
                if nxt:
                    g_again(n, q, 1, 0)
                expo(s, 4)
                if known(s + 2, B):
                    context_high(s + 2, p, it + 2)
                if nxt:
                    u_out(n, q, 1)
                expo(s, 5)
                if nxt:
                    g_again(n, q, 1, 1)
                sums_out(s, p, 1)
                if tok:
                    turned(it - 1)
                expo(s, 6)
                if known(s + 2, B):
                    g_high(s + 2, p, 0, 0)
                    g_high(s + 2, p, 0, 1)
                if tok:
                    turned_high(it - 1)
                if nxt:
                    max_in(n, q)
                expo(s, 7)

            def router_exp(part, pairs):
                act.wait_ge(left_done, part + 1)
                act.activation(score[:, pairs, :], left[:, pairs, :], ACT.Exp).then_inc(rexp_done, 1)

            def tanh_half(k, j):
                act.wait_ge(hu_filled, k + 1)
                need(act, hs_done, k - 1)
                act.activation(th[j % 2], ps[j % 2][:, :], ACT.Tanh, scale=0.5).then_inc(th_done, 1)

            def hidden_high(k, j):
                act.wait_ge(g_done, k + 1)
                need(act, y2_filled, 2 * (k - 3))
                act.activation(gh[j % 4], g[j % 4], ACT.Copy).then_inc(ghi_done, 1)

            def finish():
                sums_out(B - 1, 1, 2)
                sums_out(B - 1, 1, 3)
                rz_high(B - 1)
                tanh_half(0, 0)
                hidden_high(0, 0)
                tanh_half(1, 1)
                hidden_high(1, 1)
                tanh_half(2, 2)
                turned(PAIRS - 1)
                turned_high(PAIRS - 1)
                hidden_high(2, 2)
                router_exp(1, slice(EARLY, PAIRS))
                tanh_half(3, 3)
                hidden_high(3, 3)

                def unit(k, j, step):
                    e = 1 + 2 * step + j // CHUNKS
                    if j % CHUNKS == 2 and known(e + 1, EXPERTS):
                        weights_high(e + 1, j // CHUNKS, 2 + step)
                    tanh_half(k, j)
                    hidden_high(k, j)

                expert_loop(act, unit)

            body_loop(act, step, finish)

        @block.vector
        def _(dve):
            dve.memset(nmax[:, :, :].bitcast(F32), 0.0).then_inc(zero_done, 1)
            for q in range(2):
                dve.memset(xlm[q][C:P, :].bitcast(F32), 0.0).then_inc(zero_done, 1)
                dve.memset(mxl[q][0:C, :].bitcast(F32), 0.0).then_inc(zero_done, 1)
            def stats(b, q, i):
                need(dve, x_in[q], 16 * i)
                dve.bn_stats(bn6[q][:, :], raw_x[q][:, :]).then_inc(bn_done, 1)

            def aggregate(b, q):
                dve.bn_aggr(mv[q][:, :], bn6[q][:, :]).then_inc(stats_done, 1)

            def norm_high(b, q):
                need(dve, rstd_done, b + 1)
                need(dve, st_done, 8 * (b - 1))
                dve.tensor_scalar(xh[q][:, :], raw_x[q][:, :], mv[q][:, 0:1], rstd[q][:, 0:1], ALU.subtract, ALU.mult).then_inc(xh_done, 1)

            def norm_full(b, q):
                need(dve, xl_done, 2 * b)
                dve.tensor_scalar(xn[:, :], raw_x[q][:, :], mv[q][:, 0:1], rstd[q][:, 0:1], ALU.subtract, ALU.mult).then_inc(xn_done, 1)

            def g_low(b, q, i, odd):
                need(dve, gh_done, 4 * b + 2 * i + odd + 1)
                heads = slice(4 * i + odd, 4 * i + 4, 2)
                rows, others = slice(C * odd, C * odd + C), slice(C * (1 - odd), C * (2 - odd))
                src = ps[BANK[RING.index(f"G{i}")]][rows, :].rearrange("p (h j) -> p h j", j=N)
                dve.tensor_tensor(ghl[q][others, heads, :], src, ghl[q][rows, heads, :].bitcast(F32), ALU.subtract).then_inc(gl_done, 1)

            def maxima(b, h):
                k = RING.index(f"S{h}")
                need(dve, ring_filled, RN * b + k + 1)
                dve.tensor_reduce(nmax[:, :, C * (1 - h % 2) + h], ps[BANK[k]][:, :].rearrange("p (b j) -> p b j", j=N), AX.X, ALU.max, negate=True).then_inc(max_done, 1)

            def recip(f, half):
                cols = slice(P * half, P * half + P)
                need(dve, z_done, 2 * f + 2)
                need(dve, rzc_done, f)
                dve.reciprocal(rz[:, cols], pz[:, cols]).then_inc(recip_done, 1)

            def rz_split(f):
                need(dve, rzh_done, f + 1)
                need(dve, rb_done, 2 * f)
                dve.scalar_tensor_tensor(out=rzc[:, :], in0=rzh[:, :].bitcast(F32), scalar=kst[:, K_LOW:K_LOW + 1], in1=rz[:, :],
                                         op0=ALU.mult, op1=ALU.add).then_inc(rzc_done, 1)

            def divide(f, fp, k, bank_=pm):
                need(dve, rb_done, 2 * f + k + 1)
                need(dve, os_done, 4 * f + 2 * k + 2)
                o = os_[fp][:, 2 * k:2 * k + 2, :].rearrange("p k i -> p (k i)")
                dve.tensor_tensor(o, o, bank_[:, :], ALU.mult).then_inc(mul_done, 1)

            def residual(pair):
                need(dve, y_done, pair + 1)
                need(dve, xr_done, pair + 1)
                dve.scalar_tensor_tensor(out=x1_of(pair), in0=pm[:, 0:N], scalar=tg[:, 0:1], in1=xr[:, :],
                                         op0=ALU.mult, op1=ALU.add).then_inc(res_done, 1)

            def x1_of(pair):
                return x1[:, bass.ds(pair, 1), :].rearrange("p o d -> p (o d)")

            def token_stats(pair):
                dve.bn_stats(bn6t[:, :], x1_of(pair)).then_inc(bnt_done, 1)

            def token_aggregate():
                dve.bn_aggr(mvt[:, :], bn6t[:, :]).then_inc(statt_done, 1)

            def token_norm(pair):
                need(dve, rstdt_done, pair + 1)
                need(dve, tr_done, pair)
                dve.tensor_scalar(xn2[:, :], x1_of(pair), mvt[:, 0:1], rstdt[:, 0:1], ALU.subtract, ALU.mult).then_inc(xn2_done, 1)

            def logits_out(pair):
                need(dve, lg_filled, pair + 1)
                dve.tensor_copy(logit[:, bass.ds(pair, 1), :].rearrange("p o e -> p (o e)"), po[:, 0:E_ROUTED]).then_inc(logits_free, 1)

            def split_low(dst, src, high_done, done):
                for r in range(2):
                    dve.wait_ge(high_done, r + 1)
                    lo = dst[C:P, r:HEADS:2, :]
                    dve.tensor_tensor(lo, src[r][C:P, 0:4 * C].rearrange("p (k c) -> p k c", c=C), lo.bitcast(F32), ALU.subtract).then_inc(done, 1)

            stats(0, 0, 1)
            dve.wait_ge(bn_done, 1)
            aggregate(0, 0)
            norm_high(0, 0)
            norm_full(0, 0)
            split_low(mhl, ps, mhi_done, mhl_done)
            for odd in range(2):
                g_low(0, 0, 0, odd)
            maxima(0, 0)
            maxima(0, 1)
            split_low(nhl, pt, nhi_done, nhl_done)
            for odd in range(2):
                g_low(0, 0, 1, odd)
            for h in range(2, 6):
                maxima(0, h)
            stats(1, 1, 1)
            dve.wait_ge(bn_done, 2)
            aggregate(1, 1)
            maxima(0, 6)
            dve.wait_ge(const_in, 16)
            dve.tensor_scalar(ident_r[:, :], kst[:, K_ID:K_ID + P], 1.0, None, ALU.mult).then_inc(consts_done, 1)
            maxima(0, 7)
            dve.wait_ge(pairs_in, 16)
            dve.tensor_scalar(pair_r[:, :, :].rearrange("p k m -> p (k m)"), k_pair, 1.0, None, ALU.mult).then_inc(consts_done, 1)
            norm_high(1, 1)
            for odd in range(2):
                g_low(1, 1, 0, odd)
            norm_full(1, 1)
            dve.wait_ge(tanh_done, 1)
            dve.tensor_tensor(tgb[:, :], tg[:, 0:1], bo[:, :], ALU.mult).then_inc(tg_done, 1)
            dve.tensor_scalar(hgf[:, :], tg[:, 1:2], 0.5, None, ALU.mult).then_inc(tg_done, 1)
            dve.wait_ge(tg_done, 2)
            dve.tensor_copy(comb[:, :, E_ROUTED], hgf[:, :].broadcast_to([P, PAIRS])).then_inc(logits_free, 1)

            def step(it, p):
                s, q = 2 * it + p, 1 - p
                n, f = s + 1, s - 1
                nxt = known(n, B)
                fin = not isinstance(s, int) or s > 0
                late = not isinstance(it, int) or it > 0
                tok = p == 1 and late

                def m(*hs):
                    if nxt:
                        for h in hs:
                            maxima(n, h)
                if known(s + 2, B):
                    stats(s + 2, p, it + 2)
                m(0, 1)
                if fin:
                    recip(f, 1)
                if known(s + 2, B):
                    need(dve, bn_done, s + 3)
                if fin:
                    recip(f, 0)
                if nxt:
                    g_low(n, q, 1, 0)
                    g_low(n, q, 1, 1)
                if tok:
                    residual(it - 1)
                m(2)
                if not nxt:
                    router_first(0, slice(0, EARLY))
                if tok:
                    need(dve, res_done, it)
                if fin:
                    rz_split(f)
                if tok:
                    token_stats(it - 1)
                    need(dve, bnt_done, it)
                m(3)
                if tok:
                    token_aggregate()
                if fin:
                    divide(f, q, 0)
                m(5, 4)
                if known(s + 2, B):
                    aggregate(s + 2, p)
                if tok:
                    token_norm(it - 1)
                if fin:
                    divide(f, q, 1)
                m(6, 7)
                if known(s + 2, B):
                    norm_high(s + 2, p)
                if tok:
                    logits_out(it - 1)
                if known(s + 2, B):
                    g_low(s + 2, p, 0, 0)
                    g_low(s + 2, p, 0, 1)
                if nxt and (not known(s + 2, B)):
                    router_start(slice(0, EARLY))
                if known(s + 2, B):
                    norm_full(s + 2, p)

            router_steps = [0]

            def small(ins):
                ins.then_inc(rt_done, 1)
                router_steps[0] += 1
                dve.wait_ge(rt_done, router_steps[0])

            def wide(pairs):
                return top[:, pairs].unsqueeze(2).broadcast_to([P, pairs.stop - pairs.start, E_ROUTED])

            def router_start(pairs):
                dve.wait_ge(logits_free, pairs.stop + 1)
                small(dve.tensor_reduce(top[:, pairs], logit[:, pairs, :], AX.X, ALU.max))
                dve.tensor_tensor(left[:, pairs, :], logit[:, pairs, :], wide(pairs), ALU.subtract).then_inc(left_done, 1)

            def ranks(pairs):
                return kst[:, K_RANK:K_RANK + E_ROUTED].unsqueeze(1).broadcast_to([P, pairs.stop - pairs.start, E_ROUTED])

            def largest(src, dst, pairs):
                hit_ = hit[:, pairs, :]
                small(dve.tensor_reduce(top[:, pairs], src, AX.X, ALU.max))
                small(dve.tensor_tensor(hit_, src, wide(pairs), ALU.is_equal))
                small(dve.tensor_tensor(hit_, hit_, ranks(pairs), ALU.mult))
                small(dve.tensor_reduce(top[:, pairs], hit_, AX.X, ALU.max))
                small(dve.tensor_tensor(dst, hit_, wide(pairs), ALU.is_equal))

            def router_first(part, pairs):
                scores_ = score[:, pairs, :]
                dve.wait_ge(rexp_done, part + 1)
                small(dve.tensor_reduce(top[:, pairs], scores_, AX.X, ALU.add))
                small(dve.reciprocal(top[:, pairs], top[:, pairs]))
                small(dve.tensor_tensor(scores_, scores_, wide(pairs), ALU.mult))
                largest(scores_, pick[:, pairs, :], pairs)

            def router_second(pairs):
                scores_, left_, hit_, pick_ = (t[:, pairs, :] for t in (score, left, hit, pick))
                small(dve.scalar_tensor_tensor(out=left_, in0=pick_, scalar=-2.0, in1=scores_, op0=ALU.mult, op1=ALU.add))
                largest(left_, hit_, pairs)
                small(dve.tensor_tensor(hit_, pick_, hit_, ALU.add))
                small(dve.scalar_tensor_tensor(out=comb[:, pairs, 0:E_ROUTED], in0=hit_, scalar=hgf[:, 0:1], in1=scores_, op0=ALU.mult, op1=ALU.mult))

            def hidden(k, j):
                q, r = j % 2, j % 4
                dve.wait_ge(th_done, k + 1)
                dve.scalar_tensor_tensor(out=hs[q], in0=th[q], scalar=1.0, in1=ps[q][:, :], op0=ALU.add, op1=ALU.mult).then_inc(hs_done, 1)
                dve.wait_ge(hs_done, k + 1)
                need(dve, glo_done, k - 3)
                dve.tensor_tensor(g[r], hs[q], pt[q][:, :], ALU.mult).then_inc(g_done, 1)

            def add_expert(k, j, e):
                for half in range(2):
                    dve.wait_ge(y2_filled, 2 * k + half + 1)
                    need(dve, y2_done, 2 * k + half - 1)
                    for t in range(2):
                        tile = TILES * (j % CHUNKS) + 2 * half + t
                        mm = dve.scalar_tensor_tensor(out=x1[:, tile, :], in0=y_banks[j % 2][half][:, D * t:D * t + D],
                                                      scalar=comb[:, tile, bass.ds(e, 1)], in1=x1[:, tile, :], op0=ALU.mult, op1=ALU.add)
                    mm.then_inc(y2_done, 1)

            def finish():
                recip(B - 1, 0)
                recip(B - 1, 1)
                rz_split(B - 1)
                divide(B - 1, 1, 0, pm)
                divide(B - 1, 1, 1, pz)
                hidden(0, 0)
                router_second(slice(0, EARLY))
                hidden(1, 1)
                residual(PAIRS - 1)
                need(dve, res_done, PAIRS)
                token_stats(PAIRS - 1)
                need(dve, bnt_done, PAIRS)
                token_aggregate()
                token_norm(PAIRS - 1)
                hidden(2, 2)
                logits_out(PAIRS - 1)
                router_start(slice(EARLY, PAIRS))
                add_expert(0, 0, 0)
                router_first(1, slice(EARLY, PAIRS))
                router_second(slice(EARLY, PAIRS))
                hidden(3, 3)

                def unit(k, j, step):
                    hidden(k, j)
                    add_expert(k - LAG - 1, j + 1, 2 * step + (j + 1) // CHUNKS)

                expert_loop(dve, unit)
                for k in range(CHUNKS * EXPERTS - LAG - 1, CHUNKS * EXPERTS):
                    add_expert(k, k, EXPERTS - 1)

            body_loop(dve, step, finish)

        @block.gpsimd
        def _(pool):
            pool.memset(minus_half[:, :], -0.5).then_inc(zero_done, 1)
            pool.memset(eps[:, :], EPS).then_inc(zero_done, 1)

            def rstd_of(b, q):
                need(pool, stats_done, b + 1)
                need(pool, xn_done, b - 1)
                pool.tensor_tensor(ve[q][:, :], mv[q][:, 1:2], eps[:, :], ALU.add).then_inc(ve_done, 1)
                need(pool, ve_done, b + 1)
                pool.tensor_tensor(rstd[q][:, :], ve[q][:, :], minus_half[:, :], ALU.pow).then_inc(rstd_done, 1)

            def context_low(b, q):
                need(pool, ch_done, b + 1)
                pool.tensor_tensor(cl[q][:, :], raw_c[q][:, :], ch[q][:, :].bitcast(F32), ALU.subtract).then_inc(cl_done, 1)

            def x_low(b, q):
                need(pool, xn_done, b + 1)
                need(pool, st_done, 8 * (b - 1))
                for t, (dst, rows) in enumerate(((xlm, slice(0, C)), (mxl, slice(C, P)))):
                    pool.tensor_tensor(dst[q][rows, :], xn[rows, :], xh[q][rows, :].bitcast(F32), ALU.subtract).then_inc(xl_done, 1)
                    need(pool, xl_done, 2 * b + t + 1)

            pool.wait_ge(zero_done, 7)
            context_low(0, 0)
            rstd_of(0, 0)
            x_low(0, 0)
            context_low(1, 1)
            rstd_of(1, 1)

            def add_keys(s, h):
                need(pool, exp_done, 8 * s + h + 1)
                if h % 4 == 0:
                    need(pool, z_done, 2 * s + h // 4)
                pool.tensor_tensor(ez[h % 4][:, :], ex[h][:, 0, :], ex[h][:, 1, :], ALU.add).then_inc(ez_done, 1)

            def add_heads(f, fp, folded):
                need(pool, mul_done, 2 * f + 2)
                o = os_[fp]
                pool.tensor_tensor(o[:, 0:2, :].rearrange("p k i -> p (k i)"), o[:, 0:2, :].rearrange("p k i -> p (k i)"),
                                   o[:, 2:4, :].rearrange("p k i -> p (k i)"), ALU.add).then_inc(add_done, 1)
                need(pool, add_done, f + 1)
                need(pool, y_done, folded)
                pool.tensor_tensor(acc[fp][:, :], o[:, 0, :], o[:, 1, :], ALU.add).then_inc(sum_done, 1)

            def weights_low(e, q):
                need(pool, wh_done, e + 1)
                pool.tensor_tensor(w_lo[q][:, :], w_raw[q][:, :], w_hi[q][:, :].bitcast(F32), ALU.subtract).then_inc(wl_done, 1)

            def residual_x(it):
                pool.wait_ge(tg_done, 1)
                need(pool, xr_in, 16 * (it + 1))
                pool.tensor_tensor(xr[:, :], xr[:, :], tgb[:, :].broadcast_to([P, N]), ALU.add).then_inc(xr_done, 1)

            def token_rstd(pair):
                need(pool, statt_done, pair + 1)
                pool.tensor_tensor(vet[:, :], mvt[:, 1:2], eps[:, :], ALU.add).then_inc(vet_done, 1)
                need(pool, vet_done, pair + 1)
                need(pool, xn2_done, pair)
                pool.tensor_tensor(rstdt[:, :], vet[:, :], minus_half[:, :], ALU.pow).then_inc(rstdt_done, 1)

            def token_low(pair):
                cols = bass.ds(P * pair, P)
                need(pool, xth_done, pair + 1)
                pool.tensor_tensor(xtl[:, :, cols], xt[:, :, :], xth[:, :, cols].bitcast(F32), ALU.subtract).then_inc(xtl_done, 1)

            def step(it, p):
                s, q = 2 * it + p, 1 - p
                n, f = s + 1, s - 1
                nxt = known(n, B)
                fin = not isinstance(s, int) or s > 0
                late = not isinstance(it, int) or it > 0
                tok = p == 1 and late

                if fin:
                    for h in range(6, 8):
                        add_keys(f, h)
                add_keys(s, 0)
                if p == 0 and late:
                    residual_x(it - 1)
                if nxt:
                    x_low(n, q)
                add_keys(s, 1)
                add_keys(s, 2)
                add_keys(s, 3)
                if known(s + 2, B):
                    context_low(s + 2, p)
                if nxt and (not known(s + 2, B)):
                    weights_low(0, 0)
                if tok:
                    token_rstd(it - 1)
                for h in range(4, 6):
                    add_keys(s, h)
                if known(s + 2, B):
                    rstd_of(s + 2, p)
                if fin:
                    add_heads(f, q, it if p == 1 else it - 1)
                if tok:
                    token_low(it - 1)

            def hidden_low(k, j):
                pool.wait_ge(ghi_done, k + 1)
                need(pool, y2_filled, 2 * (k - 3))
                pool.tensor_tensor(gl[j % 4], g[j % 4], gh[j % 4].bitcast(F32), ALU.subtract).then_inc(glo_done, 1)

            def finish():
                for h in range(6, 8):
                    add_keys(B - 1, h)
                residual_x(PAIRS - 1)
                weights_low(1, 1)
                add_heads(B - 1, 1, PAIRS - 1)
                hidden_low(0, 0)
                token_rstd(PAIRS - 1)
                hidden_low(1, 1)
                token_low(PAIRS - 1)
                hidden_low(2, 2)
                hidden_low(3, 3)

                def unit(k, j, step):
                    e = 1 + 2 * step + j // CHUNKS
                    if j % CHUNKS == 2 and known(e + 1, EXPERTS):
                        weights_low(e + 1, j // CHUNKS)
                    hidden_low(k, j)

                expert_loop(pool, unit)

            body_loop(pool, step, finish)


def kernel(**inputs):
    from concourse import bacc
    from concourse.bass_utils import run_bass_kernel_spmd

    def get(name):
        return np.ascontiguousarray(inputs[name])

    w1 = np.concatenate([get("L0_ffn_w1"), get("L0_ffn_ws1")[None]])
    w3 = np.concatenate([get("L0_ffn_w3"), get("L0_ffn_ws3")[None]])
    w2 = np.concatenate([get("L0_ffn_w2"), get("L0_ffn_ws2")[None]])
    w13T = np.stack([w1, w3], axis=1).reshape(EXPERTS, 2, INTER, DB, P).transpose(0, 4, 1, 3, 2).reshape(EXPERTS, P, -1)
    w2T = w2.transpose(0, 2, 1)
    arrays = {
        "x": get("x"), "ctx_in": get("ctx_2048"), "g_xattn": get("g_xattn"), "g_ffn": get("g_ffn"),
        "wq": get("L0_xattn_Wq"), "wk": get("L0_xattn_Wkv")[:HEADS * DH], "wv": get("L0_xattn_Wkv")[HEADS * DH:],
        "woT": get("L0_xattn_Wout").T, "bout": get("L0_xattn_bout"), "gateT": get("L0_ffn_gate_w").T,
        "w_all": np.concatenate([w13T, w2T], axis=2), "consts": constants(),
    }
    arrays = {f"in_{k}": np.ascontiguousarray(a) for k, a in arrays.items()}
    nc = bacc.Bacc("TRN2", target_bir_lowering=False, num_devices=1)
    args = [nc.dram_tensor(k, a.shape, mybir.dt.from_np(a.dtype), kind="ExternalInput").ap() for k, a in arrays.items()]
    out = nc.dram_tensor("out", (B, C, N), F32, kind="ExternalOutput").ap()
    build(nc, *args, out)
    r = run_bass_kernel_spmd(nc, [arrays], core_ids=[0])
    return r.results[0]["out"]
```
